# Optimizing a Trainium2 kernel written in Bass

```python
import numpy as np
import jax
import jax.numpy as jnp

def _softmax(x, axis=-1):
    return jax.nn.softmax(x, axis=axis)

def _gelu(x):
    return jax.nn.gelu(x, approximate=True)

def _silu(x):
    return jax.nn.silu(x)

def _sigmoid(x):
    return jax.nn.sigmoid(x)

def _layernorm(x, axis=-1, eps=1e-05):
    m = jnp.mean(x, axis=axis, keepdims=True)
    v = jnp.var(x, axis=axis, keepdims=True)
    return (x - m) / jnp.sqrt(v + eps)

def _scatter_add(tgt, idx, src, axis=0):
    return tgt.at[idx].add(src)

def _segment_sum(src, seg, n):
    return jax.ops.segment_sum(src, seg, n)
kernel_name = 'mk_conv_attn_hybrid_d2_conv_nchw512_r4_e61d72'

def setup_inputs(seed: int=0):
    np.random.seed(seed)
    _w = jnp.asarray

    def _rec_inputs():
        import jax
        import jax.numpy as jnp
        _gk = jax.random.key(seed)
        x = -0.0003929 + 0.9999 * jax.random.normal(jax.random.fold_in(_gk, 1), (32, 128, 32, 32), jnp.float32)
        return x
    x = _rec_inputs()

    def _L0_conv_setup():
        import jax, jax.numpy as jnp
        import numpy as np
        GROUPS = 8
        N_HEADS = 1
        EPS = 1e-05

        def group_norm(x, gamma, beta):
            B, C, H, W = x.shape
            xg = x.reshape(B, GROUPS, C // GROUPS, H, W)
            mu = xg.mean(axis=(2, 3, 4), keepdims=True)
            var = xg.var(axis=(2, 3, 4), keepdims=True)
            xn = ((xg - mu) * jax.lax.rsqrt(var + EPS)).reshape(B, C, H, W)
            return xn * gamma[None, :, None, None] + beta[None, :, None, None]
        key = jax.random.key(seed)
        ks = jax.random.split(key, 7)
        C = 128
        B, H, W = (32, 32, 32)
        s_in = 1.0 / np.sqrt(C)
        return {'x': jax.random.normal(ks[0], (B, C, H, W), dtype=jnp.float32), 'norm_w': jnp.ones((C,), dtype=jnp.float32), 'norm_b': jnp.zeros((C,), dtype=jnp.float32), 'qkv_w': jax.random.uniform(ks[1], (3 * C, C), jnp.float32, -s_in, s_in), 'qkv_b': jax.random.uniform(ks[2], (3 * C,), jnp.float32, -s_in, s_in), 'proj_w': jax.random.uniform(ks[3], (C, C), jnp.float32, -s_in, s_in), 'proj_b': jax.random.uniform(ks[4], (C,), jnp.float32, -s_in, s_in)}
    _L0_conv_all = _L0_conv_setup()
    _L0_conv_in = {k: v for k, v in _L0_conv_all.items() if k in ('norm_w', 'norm_b', 'qkv_w', 'qkv_b', 'proj_w', 'proj_b')}
    del _L0_conv_all

    def _L1_attn_setup():
        import jax, jax.numpy as jnp
        import numpy as np
        S, R, DH = (8, 2, 16)
        key = jax.random.key(seed)
        ks = jax.random.split(key, 7)
        b, n, dim = (2, 512, 128)

        def w(k, i, o):
            return jax.random.normal(k, (i, o), dtype=jnp.float32) / np.sqrt(i)
        return {'x': jax.random.normal(ks[0], (b, n, dim), dtype=jnp.float32), 'wq_s': w(ks[1], dim, S * DH), 'wk_s': w(ks[2], dim, S * DH), 'wv_r': w(ks[3], dim, R * DH), 'wq_r': w(ks[4], dim, S * DH), 'wk_ret': w(ks[5], DH, DH), 'w_out': w(ks[6], S * DH, dim)}
    _L1_attn_all = _L1_attn_setup()
    _L1_attn_in = {k: v for k, v in _L1_attn_all.items() if k in ('wq_s', 'wk_s', 'wv_r', 'wq_r', 'wk_ret', 'w_out')}
    del _L1_attn_all

    def _L1_ffn_setup():
        import jax, jax.numpy as jnp
        import numpy as np
        BLOCK = 16
        NF4_TABLE = jnp.array([-1.0, -0.6961928009986877, -0.5250730514526367, -0.39491748809814453, -0.28444138169288635, -0.18477343022823334, -0.09105003625154495, 0.0, 0.07958029955625534, 0.16093020141124725, 0.24611230194568634, 0.33791524171829224, 0.44070982933044434, 0.5626170039176941, 0.7229568362236023, 1.0], dtype=jnp.float32)

        def _dequant_nf4(qidx, scales):
            w = NF4_TABLE[qidx].reshape(-1, BLOCK) * scales[:, None]
            return w.reshape(qidx.shape)
        key = jax.random.key(seed)
        k1, k2, k3, k4 = jax.random.split(key, 4)
        x = jax.random.normal(k1, (4, 2048, 128), dtype=jnp.float32)
        qidx = jax.random.randint(k2, (128, 128), 0, 16, dtype=jnp.int32)
        scales = jax.random.uniform(k3, (1024,), dtype=jnp.float32)
        W = jax.random.normal(k4, (128, 128), dtype=jnp.float32) * (1.0 / np.sqrt(512.0))
        return {'x': x, 'qidx': qidx, 'scales': scales, 'W': W}
    _L1_ffn_all = _L1_ffn_setup()
    _L1_ffn_in = {k: v for k, v in _L1_ffn_all.items() if k in ('qidx', 'scales', 'W')}
    del _L1_ffn_all
    return {'x': x, 'L0_conv_norm_w': _L0_conv_in['norm_w'], 'L0_conv_norm_b': _L0_conv_in['norm_b'], 'L0_conv_qkv_w': _L0_conv_in['qkv_w'], 'L0_conv_qkv_b': _L0_conv_in['qkv_b'], 'L0_conv_proj_w': _L0_conv_in['proj_w'], 'L0_conv_proj_b': _L0_conv_in['proj_b'], 'L1_attn_wq_s': _L1_attn_in['wq_s'], 'L1_attn_wk_s': _L1_attn_in['wk_s'], 'L1_attn_wv_r': _L1_attn_in['wv_r'], 'L1_attn_wq_r': _L1_attn_in['wq_r'], 'L1_attn_wk_ret': _L1_attn_in['wk_ret'], 'L1_attn_w_out': _L1_attn_in['w_out'], 'L1_ffn_qidx': _L1_ffn_in['qidx'], 'L1_ffn_scales': _L1_ffn_in['scales'], 'L1_ffn_W': _L1_ffn_in['W']}

def reference(x, L0_conv_norm_w, L0_conv_norm_b, L0_conv_qkv_w, L0_conv_qkv_b, L0_conv_proj_w, L0_conv_proj_b, L1_attn_wq_s, L1_attn_wk_s, L1_attn_wv_r, L1_attn_wq_r, L1_attn_wk_ret, L1_attn_w_out, L1_ffn_qidx, L1_ffn_scales, L1_ffn_W):
    import jax
    import jax.numpy as jnp

    def _L0_conv_ref(x, norm_w, norm_b, qkv_w, qkv_b, proj_w, proj_b):
        import jax, jax.numpy as jnp
        import numpy as np
        GROUPS = 8
        N_HEADS = 1
        EPS = 1e-05

        def group_norm(x, gamma, beta):
            B, C, H, W = x.shape
            xg = x.reshape(B, GROUPS, C // GROUPS, H, W)
            mu = xg.mean(axis=(2, 3, 4), keepdims=True)
            var = xg.var(axis=(2, 3, 4), keepdims=True)
            xn = ((xg - mu) * jax.lax.rsqrt(var + EPS)).reshape(B, C, H, W)
            return xn * gamma[None, :, None, None] + beta[None, :, None, None]
        B, C, H, W = x.shape
        h = group_norm(x, norm_w, norm_b)
        qkv = jnp.einsum('bchw,oc->bohw', h, qkv_w) + qkv_b[None, :, None, None]
        q, k, v = jnp.split(qkv, 3, axis=1)
        to_tok = lambda t: t.reshape(B, C, H * W).transpose(0, 2, 1)
        q, k, v = (to_tok(q), to_tok(k), to_tok(v))
        scale = (C // N_HEADS) ** (-0.5)
        attn = jax.nn.softmax(jnp.einsum('bnc,bmc->bnm', q, k) * scale, axis=-1)
        out = jnp.einsum('bnm,bmc->bnc', attn, v)
        out = out.transpose(0, 2, 1).reshape(B, C, H, W)
        out = jnp.einsum('bchw,oc->bohw', out, proj_w) + proj_b[None, :, None, None]
        return x + out

    def _L1_attn_ref(x, wq_s, wk_s, wv_r, wq_r, wk_ret, w_out):
        import jax, jax.numpy as jnp
        import numpy as np
        S, R, DH = (8, 2, 16)
        b, n, dim = x.shape
        scale = DH ** (-0.5)
        sq = (x @ wq_s).reshape(b, n, S, DH).transpose(0, 2, 1, 3) * scale
        sk = (x @ wk_s).reshape(b, n, S, DH).transpose(0, 2, 1, 3)
        rv = (x @ wv_r).reshape(b, n, R, DH).transpose(0, 2, 1, 3)
        search_sim = jnp.einsum('bsid,bsjd->bsij', sq, sk)
        search_attn = jax.nn.softmax(search_sim, axis=-1)
        retrieved = jnp.einsum('bsij,brjd->bsird', search_attn, rv)
        rq = (x @ wq_r).reshape(b, n, S, DH).transpose(0, 2, 1, 3) * scale
        rk = retrieved @ wk_ret
        retrieval_sim = jnp.einsum('bsid,bsird->bsir', rq, rk)
        retrieval_attn = jax.nn.softmax(retrieval_sim, axis=-1)
        out = jnp.einsum('bsir,bsird->bsid', retrieval_attn, retrieved)
        out = out.transpose(0, 2, 1, 3).reshape(b, n, S * DH)
        return out @ w_out

    def _L1_ffn_ref(x, qidx, scales, W):
        import jax, jax.numpy as jnp
        import numpy as np
        BLOCK = 16
        NF4_TABLE = jnp.array([-1.0, -0.6961928009986877, -0.5250730514526367, -0.39491748809814453, -0.28444138169288635, -0.18477343022823334, -0.09105003625154495, 0.0, 0.07958029955625534, 0.16093020141124725, 0.24611230194568634, 0.33791524171829224, 0.44070982933044434, 0.5626170039176941, 0.7229568362236023, 1.0], dtype=jnp.float32)

        def _dequant_nf4(qidx, scales):
            w = NF4_TABLE[qidx].reshape(-1, BLOCK) * scales[:, None]
            return w.reshape(qidx.shape)
        w_lora = _dequant_nf4(qidx, scales)
        y = jnp.einsum('bsd,od->bso', x, w_lora)
        out = jnp.einsum('bsd,od->bso', y, W)
        return out

    def _gn(v, G=32, eps=1e-05):
        B_, C_, H_, W_ = v.shape
        g = v.reshape(B_, G, C_ // G, H_, W_)
        m = jnp.mean(g, axis=(2, 3, 4), keepdims=True)
        s = jnp.var(g, axis=(2, 3, 4), keepdims=True)
        return ((g - m) / jnp.sqrt(s + eps)).reshape(v.shape)

    def _ln_c(v, eps=1e-06):
        m = jnp.mean(v, axis=1, keepdims=True)
        s = jnp.var(v, axis=1, keepdims=True)
        return (v - m) / jnp.sqrt(s + eps)

    def _ln_t(v, eps=1e-05):
        m = jnp.mean(v, axis=-1, keepdims=True)
        s = jnp.var(v, axis=-1, keepdims=True)
        return (v - m) / jnp.sqrt(s + eps)

    def _to_tokens(v):
        B_, C_, H_, W_ = v.shape
        return v.reshape(B_, C_, H_ * W_).transpose(0, 2, 1)

    def _from_tokens(t, like):
        B_, C_, H_, W_ = like.shape
        return t.transpose(0, 2, 1).reshape(B_, C_, H_, W_)
    x = _L0_conv_ref(x, L0_conv_norm_w, L0_conv_norm_b, L0_conv_qkv_w, L0_conv_qkv_b, L0_conv_proj_w, L0_conv_proj_b)
    t = _to_tokens(x)
    t = t + _L1_attn_ref(_ln_t(t), L1_attn_wq_s, L1_attn_wk_s, L1_attn_wv_r, L1_attn_wq_r, L1_attn_wk_ret, L1_attn_w_out)
    t = t + _L1_ffn_ref(_ln_t(t), L1_ffn_qidx, L1_ffn_scales, L1_ffn_W)
    x = _from_tokens(t, x)
    return x

_drawn_inputs = setup_inputs


def setup_inputs(seed=0):
    import zlib

    import numpy as np

    out = dict(_drawn_inputs(seed))
    spreads = {'L0_conv_norm_w': (1.0, 0.6), 'L0_conv_norm_b': (0.0, 0.1)}
    factors = {'L1_attn_wq_r': 7.628, 'L1_attn_wk_ret': 7.477}
    for name, (base, spread) in spreads.items():
        noise = np.random.default_rng([zlib.crc32(name.encode()), seed]).standard_normal(out[name].shape)
        drawn = base * np.exp(spread * noise) if base else spread * noise
        out[name] = jnp.asarray(drawn.astype(out[name].dtype))
    for name, factor in factors.items():
        out[name] = (out[name] * factor).astype(out[name].dtype)
    return out
```

```python
from contextlib import ExitStack

import numpy as np

import concourse.bass as bass
from concourse import mybir

F32 = mybir.dt.float32
F32R = mybir.dt.float32r
I32 = mybir.dt.int32
ALU = mybir.AluOpType
ACT = mybir.ActivationFunctionType
AXIS = mybir.AxisListType

P = 128
HALF = 512
HEADS = 8
HEAD_DIM = 16
RETRIEVERS = 2
PAIRS = HEADS // 2
GROUP = 4
QUAD = 32
GROUPS_L0 = 8
EPS = 1e-5
EXP_ARG_MAX = 80.0
NF4 = [-1.0, -0.6961928009986877, -0.5250730514526367, -0.39491748809814453, -0.28444138169288635,
       -0.18477343022823334, -0.09105003625154495, 0.0, 0.07958029955625534, 0.16093020141124725,
       0.24611230194568634, 0.33791524171829224, 0.44070982933044434, 0.5626170039176941,
       0.7229568362236023, 1.0]
NF4_BLOCK = 16

LINKS_PER_IMAGE = {True: 67, False: 0}

BANKS_OF = {
    "norm_group_mean": 1, "norm_group_var": 1, "norm_apply": 0, "q0": 2, "k0": 2, "v0": 2,
    "max0": 18, "score0": 2, "x_tokens": 2, "value0": 1, "ln1": 0, "ln1_channels": 2, "q1": 2,
    "k1": 2, "rv": 2, "expand": 4, "max1": 34, "rqk": 2, "den": 0, "evict_u": 0,
    "retrieve_a": 2, "retrieve_b": 0, "mixed_channels": 2, "out1": 2, "ln2": 0, "ln2_channels": 2,
    "ffn": 2, "take_tokens": 0, "take_values": 0, "result": 2,
}


def schedule(general):
    steps = [[] for _ in range(32)]

    def put(step, kind, stage, arg=0):
        steps[step].append((kind, stage, arg))

    def expand(step, kind, pair):
        put(step, kind, "expand", pair)
        if general:
            put(step, kind, "max1", pair)

    put(0, "HEAD", "take_values")
    put(0, "TAIL", "evict_u", 3)
    put(0, "FRONT", "norm_group_mean")
    expand(0, "HEAD", 2)
    put(1, "TAIL", "den", 3)
    put(1, "FRONT", "norm_group_var")
    expand(1, "HEAD", 3)
    put(2, "FRONT", "norm_apply")
    put(3, "TAIL", "retrieve_a", 3)
    put(3, "FRONT", "q0")
    put(4, "FRONT", "k0")
    if general:
        put(4, "FRONT", "max0")
    put(5, "TAIL", "retrieve_b", 3)
    put(5, "HEAD", "rqk")
    put(5, "FRONT", "v0")
    for n in range(8):
        put(6 + n, "FRONT", "score0", n)
    put(6, "TAIL", "mixed_channels")
    put(7, "TAIL", "out1")
    put(8, "TAIL", "ln2")
    put(8, "HEAD", "evict_u", 0)
    put(9, "HEAD", "den", 0)
    put(10, "TAIL", "ln2_channels")
    put(11, "HEAD", "retrieve_a", 0)
    put(11, "TAIL", "ffn")
    put(12, "TAIL", "result")
    put(13, "HEAD", "retrieve_b", 0)
    put(13, "HEAD", "take_tokens")
    put(13, "FRONT", "x_tokens")
    put(16, "HEAD", "evict_u", 1)
    put(17, "HEAD", "den", 1)
    for n in range(8):
        put(14 + n, "FRONT", "value0", n)
    put(19, "HEAD", "retrieve_a", 1)
    put(21, "HEAD", "retrieve_b", 1)
    put(22, "FRONT", "ln1")
    put(24, "FRONT", "ln1_channels")
    put(24, "HEAD", "evict_u", 2)
    put(25, "HEAD", "den", 2)
    put(25, "FRONT", "q1")
    put(26, "FRONT", "k1")
    put(27, "HEAD", "retrieve_a", 2)
    put(27, "FRONT", "rv")
    expand(28, "FRONT", 0)
    put(29, "HEAD", "retrieve_b", 2)
    expand(29, "FRONT", 1)
    return steps


class Banks:

    def __init__(self):
        self.taken = 0
        self.looped = 0

    def take(self):
        bank, before = self.taken % 2, self.taken // 2 + self.looped
        self.taken += 1
        return bank, before

    def skip(self, stage):
        self.taken += BANKS_OF[stage]


class Links:

    def __init__(self, sem):
        self.sem = sem
        self.count = 0
        self.looped = 0

    def next(self):
        self.count += 1
        return self.count + self.looped


def wait(engine, sem, value):
    if not isinstance(value, int) or value > 0:
        engine.wait_ge(sem, value)


def in_order(engine, steps, images, attend, stages, banks, links, links_per_image, first=None, after=None):

    def behind(step, kinds, b):
        for kind, stage, arg in steps[step]:
            if kind in kinds:
                image = b + {"HEAD": 0, "TAIL": -1, "FRONT": 1}[kind]
                if stage in stages:
                    stages[stage](image, arg)
                elif banks:
                    banks.skip(stage)

    def image_of(b, kinds):
        if first:
            first(b)
        for step in range(len(steps)):
            attend(b, step)
            behind(step, kinds, b)
            if after:
                after(b, step)

    for step in range(len(steps)):
        behind(step, ("FRONT",), -1)
    image_of(0, ("HEAD", "FRONT"))
    banks_per_image = sum(BANKS_OF[stage] for step in steps for _, stage, _ in step)
    before = links.count if links else 0
    with engine.Fori(1, images - 1) as b:
        if banks:
            banks.looped = (b - 1) * (banks_per_image // 2)
        if links:
            links.looped = (b - 1) * links_per_image
        image_of(b, ("HEAD", "TAIL", "FRONT"))
    if links:
        assert links.count - before == links_per_image, links.count - before
        links.looped = (images - 3) * links_per_image
    if banks:
        banks.looped = (images - 3) * (banks_per_image // 2)
    image_of(images - 1, ("HEAD", "TAIL"))
    for step in range(len(steps)):
        behind(step, ("TAIL",), images)


def build(nc, x, norm_w, norm_b, qkv_w, qkv_b, proj_w, proj_b, wq_s, wk_s, wv_r, wq_r, wk_ret, w_out,
          qidx, scales, ffn_w, y):
    images, _, height, width = x.shape
    tokens = height * width
    tiles = tokens // P
    halves = tokens // HALF
    tiles_per_half = HALF // P
    scale0 = float(P) ** -0.5
    scale1 = float(HEAD_DIM) ** -0.5
    ring = 4
    phases = (HEADS // GROUP) * halves
    steps_per_image = phases * tiles
    adds = tiles - 1
    x_dram = x.rearrange("b c h w -> b c (h w)")
    y_dram = y.rearrange("b c h w -> b c (h w)")

    with ExitStack() as ctx:
        def sb(name, shape, dtype=F32):
            return ctx.enter_context(nc.sbuf_tensor(name, shape, dtype))

        def psum(name, shape):
            return ctx.enter_context(nc.psum_tensor(name, shape, F32))

        def sem(name):
            return ctx.enter_context(nc.semaphore(name))

        ps_score = psum("ps_score", [P, 2, 2, HALF])
        ps_u = psum("ps_u", [P, HALF])
        ps_den = psum("ps_den", [P, HALF])
        ps_bank = psum("ps_bank", [P, 2, HALF])

        ident = sb("ident", [P, P])
        group_mean = sb("group_mean", [P, P])
        ones = sb("ones", [P, P])
        head_rows = sb("head_rows", [P, 2])
        q_of_hi = sb("q_of_hi", [P, PAIRS, P], F32R)
        q_of_lo = sb("q_of_lo", [P, PAIRS, P], F32R)
        k_of_hi = sb("k_of_hi", [P, PAIRS, P], F32R)
        k_of_lo = sb("k_of_lo", [P, PAIRS, P], F32R)
        first_row = sb("first_row", [P, P], F32R)

        p0 = sb("p0", [P, tiles, tokens])
        setup_tiles = p0[:, :, :].rearrange("p a (b n) -> p (a b) n", n=P)
        qkv_rows = setup_tiles[:, 0:3, :]
        proj_rows, ffn_rows, wq_r_sb, wk_ret_blocks = (setup_tiles[:, n, :] for n in range(3, 7))
        bias_v, proj_bias, q_value, lora, lora_part = (setup_tiles[:, n, :] for n in range(7, 12))
        q_index = setup_tiles[:, 12, :].bitcast(I32)
        turned = setup_tiles[:, 13:17, :]
        qk_w = sb("qk_w", [P, 2, P])
        value_w = sb("value_w", [P, P])
        token_bias = sb("token_bias", [P, P])
        gate_w = sb("gate_w", [P, P])
        ffn_w_sb = sb("ffn_w_sb", [P, P])
        wq_sb = sb("wq_sb", [P, P])
        wk_sb = sb("wk_sb", [P, P])
        wv_r_sb = sb("wv_r_sb", [P, RETRIEVERS * HEAD_DIM])
        wv_sb = sb("wv_sb", [P, 4, QUAD])
        w_out_sb = sb("w_out_sb", [P, P])
        norm_cols = sb("norm_cols", [P, 2])
        qkv_bias = sb("qkv_bias", [P, 3])
        block_scale = sb("block_scale", [P, P // NF4_BLOCK])
        minus_half = sb("minus_half", [P, 8])

        x_sb = sb("x_sb", [P, tokens])
        stat0 = sb("stat0", [P, 2, 6])
        moment0 = sb("moment0", [P, 12])
        work = sb("work", [P, tokens])
        q_hi = sb("q_hi", [P, tokens], F32R)
        q_lo = sb("q_lo", [P, tokens], F32R)
        k_hi = sb("k_hi", [P, tokens], F32R)
        k_lo = sb("k_lo", [P, tokens], F32R)
        v0 = sb("v0", [P, tiles, P + 1])
        den0 = sb("den0", [P, 2, tiles])
        t_front = sb("t_front", [P, tiles, P])
        t_core = sb("t_core", [P, tiles, P])

        stat1 = sb("stat1", [P, tiles, 6])
        moment1 = sb("moment1", [P, 8, tiles])
        channels = sb("channels", [P, tokens])
        q_stack = sb("q_stack", [P, PAIRS, tokens], F32R)
        k_stack = sb("k_stack", [P, HEADS, tokens], F32R)
        rv_next = sb("rv_next", [P, tiles, QUAD])
        rv = sb("rv", [P, tiles, QUAD])
        rqk = sb("rqk", [P, tiles, P])
        p1 = sb("p1", [P, ring, GROUP, HALF])
        p_sum = sb("p_sum", [P, GROUP, HALF])
        u_sb = sb("u_sb", [P, HALF])
        den_sb = sb("den_sb", [P, HALF])
        u_tok = sb("u_tok", [P, tiles_per_half, GROUP, QUAD])
        den_tok = sb("den_tok", [P, tiles_per_half * GROUP])
        small = sb("small", [P, 6, tiles_per_half * GROUP])
        prod = sb("prod", [P, 2, tiles_per_half * GROUP, HEAD_DIM])
        work_tok = work[:, :].rearrange("p (i c) -> p i c", c=P)
        start_mark = sb("start_mark", [P, 2])
        part_dev = sb("part_dev", [P, 2 * halves])
        range_seen = sb("range_seen", [P, 2, tiles_per_half * GROUP])
        max_part = sb("max_part", [P, 2, halves, tiles])
        max_both = sb("max_both", [P, 2, tiles])
        max_cols = sb("max_cols", [P, tiles, P])
        max_row = sb("max_row", [P, tokens], F32R)
        mixed = sb("mixed", [P, tiles, P])
        out_sb = sb("out_sb", [P, tokens])

        weights_loaded = sem("weights_loaded")
        blocks_zeroed = sem("blocks_zeroed")
        pool_ready = sem("pool_ready")
        pool_link = sem("pool_link")
        turned_filled = sem("turned_filled")
        turned_ready = sem("turned_ready")
        folded_filled = sem("folded_filled")
        dve_setup = sem("dve_setup")
        weights_ready = sem("weights_ready")

        with nc.Block() as block:
            @block.sync
            def _(sp):
                loads = [
                    (qkv_rows, qkv_w.rearrange("(t o) c -> o t c", o=P)),
                    (proj_rows, proj_w), (ffn_rows, ffn_w), (wq_r_sb, wq_r),
                    (wq_sb[:, :], wq_s), (wk_sb[:, :], wk_s), (wv_r_sb[:, :], wv_r),
                    (w_out_sb[:, :], w_out), (q_index, qidx),
                    (block_scale[:, :], scales.rearrange("(o k) -> o k", o=P)),
                    (norm_cols[:, 0:1], norm_w.rearrange("(c a) -> c a", a=1)),
                    (norm_cols[:, 1:2], norm_b.rearrange("(c a) -> c a", a=1)),
                    (proj_bias, proj_b.partition_broadcast(P)),
                ]
                for to, source in loads:
                    sp.dma_start(to, source).then_inc(weights_loaded, 16)
                with nc.allow_non_contiguous_dma(reason="384 biases, once"):
                    sp.dma_start(qkv_bias[:, :], qkv_b.rearrange("(t o) -> o t", o=P)).then_inc(weights_loaded, 16)
                sp.wait_ge(blocks_zeroed, 1)
                for h in range(HEADS):
                    rows = slice(h * HEAD_DIM, (h + 1) * HEAD_DIM)
                    sp.dma_start(wk_ret_blocks[rows, rows], wk_ret).then_inc(weights_loaded, 16)

            @block.gpsimd
            def _(pool):
                links = Links(pool_link)

                def link(instruction):
                    instruction.then_inc(links.sem, 1)
                    pool.wait_ge(links.sem, links.next())

                pool.memset(wk_ret_blocks, 0.0).then_inc(blocks_zeroed, 1)
                pool.memset(minus_half[:, :], -0.5)
                pool.memset(ones[:, :], 1.0)
                link(pool.memset(ident[:, :], 0.0))
                link(pool.affine_select(out=ident[:, :], in_=ident[:, :], compare_op=ALU.not_equal, fill=1.0,
                                        base=0, pattern=[[-1, P]], channel_multiplier=1))
                size = P // GROUPS_L0
                blocks = group_mean[:, :].rearrange("p (g c) -> p g c", g=GROUPS_L0)
                link(pool.memset(group_mean[:, :], 1.0 / size))
                link(pool.affine_select(out=blocks, in_=blocks, compare_op=ALU.is_ge, fill=0.0, base=0,
                                        pattern=[[-size, GROUPS_L0], [0, size]], channel_multiplier=1))
                link(pool.affine_select(out=blocks, in_=blocks, compare_op=ALU.is_ge, fill=0.0, base=size - 1,
                                        pattern=[[size, GROUPS_L0], [0, size]], channel_multiplier=-1))
                pool.memset(v0[:, :, P:P + 1], 1.0).then_inc(pool_ready, 1)
                pool.wait_ge(weights_loaded, 16 * (14 + HEADS))
                link(pool.tensor_copy(q_value, q_index))
                link(pool.memset(lora, 0.0))
                for n, value in enumerate(NF4):
                    link(pool.tensor_scalar(lora_part, q_value, float(n), float(value),
                                            ALU.is_equal, ALU.mult))
                    link(pool.tensor_tensor(lora, lora, lora_part, ALU.add))
                pool.tensor_tensor(lora.rearrange("p (k j) -> p k j", j=NF4_BLOCK),
                                   lora.rearrange("p (k j) -> p k j", j=NF4_BLOCK),
                                   block_scale[:, :].unsqueeze(2).broadcast_to([P, P // NF4_BLOCK, NF4_BLOCK]),
                                   ALU.mult).then_inc(pool_ready, 1)

            @block.tensor
            def _(pe):
                scratch = ps_score[:, :, :, :].rearrange("p a b n -> p (a b n)")
                pe.wait_ge(pool_ready, 1)
                pe.wait_ge(weights_loaded, 16 * (14 + HEADS))
                for n, source in enumerate((qkv_rows[:, 0, :], qkv_rows[:, 1, :], proj_rows,
                                            ffn_rows, wq_r_sb, wk_ret_blocks)):
                    last = pe.transpose(scratch[:, n * P:(n + 1) * P], source, ident[:, :])
                last.then_inc(turned_filled, 1)
                pe.wait_ge(turned_ready, 1)
                pe.wait_ge(pool_ready, 2)
                for n, (left, right) in enumerate((
                        (qkv_rows[:, 2, :], turned[:, 0, :]),
                        (bias_v, turned[:, 0, :]),
                        (turned[:, 2, :], turned[:, 3, :]),
                        (lora, turned[:, 1, :]))):
                    last = pe.matmul(ps_bank[:, 0, n * P:(n + 1) * P], left, right, start=True, stop=True)
                last.then_inc(folded_filled, 1)

            @block.vector
            def _(dve):
                links = Links(dve_setup)

                def link(instruction):
                    instruction.then_inc(links.sem, 1)
                    dve.wait_ge(links.sem, links.next())

                dve.memset(q_of_hi[:, :, :].bitcast(F32), 0.0)
                dve.memset(q_of_lo[:, :, :].bitcast(F32), 0.0)
                dve.memset(k_of_hi[:, :, :].bitcast(F32), 0.0)
                dve.memset(max_cols[:, :, :], 0.0)
                dve.memset(range_seen[:, :, :], 0.0)
                link(dve.memset(k_of_lo[:, :, :].bitcast(F32), 0.0))
                dve.wait_ge(pool_ready, 1)
                pairs = ident[:, :].rearrange("p (a r) -> p a r", r=QUAD)
                for to, part in ((q_of_hi, 0), (q_of_hi, 1), (q_of_lo, 2), (k_of_hi, 0), (k_of_lo, 1), (k_of_hi, 2)):
                    dve.tensor_copy(to[:, :, part * QUAD:(part + 1) * QUAD], pairs)
                dve.tensor_copy(first_row[:, :], ident[:, 0:1].broadcast_to([P, P]))
                for n in range(2):
                    rows = ident[:, 0:3 * QUAD].rearrange("p (a h d) -> p a h d", a=3, h=2)[:, :, n, :]
                    dve.tensor_reduce(head_rows[:, n:n + 1], rows, AXIS.XY, ALU.add)
                dve.wait_ge(weights_loaded, 16 * (14 + HEADS))
                dve.tensor_scalar(bias_v, ones[:, :], qkv_bias[:, 2:3], None, ALU.mult)
                for n in range(4):
                    dve.tensor_copy(wv_sb[:, n, 0:HEAD_DIM], wv_r_sb[:, HEAD_DIM:])
                    dve.tensor_tensor(wv_sb[:, n, HEAD_DIM:], wv_r_sb[:, 0:HEAD_DIM], wv_r_sb[:, HEAD_DIM:],
                                      ALU.subtract)
                dve.wait_ge(turned_filled, 1)
                scratch = ps_score[:, :, :, :].rearrange("p a b n -> p (a b n)")
                dve.tensor_copy(qk_w[:, :, :].rearrange("p a n -> p (a n)"), scratch[:, 0:2 * P])
                dve.tensor_copy(turned.rearrange("p a n -> p (a n)"), scratch[:, 2 * P:6 * P])\
                   .then_inc(turned_ready, 1)
                dve.wait_ge(folded_filled, 1)
                dve.tensor_copy(value_w[:, :], ps_bank[:, 0, 0:P])
                dve.tensor_tensor(token_bias[:, :], ps_bank[:, 0, P:2 * P], proj_bias, ALU.add)
                dve.tensor_copy(gate_w[:, :], ps_bank[:, 0, 2 * P:3 * P])
                dve.tensor_copy(ffn_w_sb[:, :], ps_bank[:, 0, 3 * P:4 * P]).then_inc(weights_ready, 1)

        def one_pass(general):
            tag = "g_" if general else "f_"
            steps = schedule(general)
            links_per_image = LINKS_PER_IMAGE[general]

            x_loaded = sem(tag + "x_loaded")
            stored = sem(tag + "stored")
            bank_filled = [sem(tag + "bank0_filled"), sem(tag + "bank1_filled")]
            mean_read = sem(tag + "mean_read")
            value0_added = sem(tag + "value0_added")
            rqk_ready = sem(tag + "rqk_ready")
            den_tok_ready = sem(tag + "den_tok_ready")
            out1_added = sem(tag + "out1_added")
            dve_link = sem(tag + "dve_link")
            moments_ready = sem(tag + "moments_ready")
            spread_ready = sem(tag + "spread_ready")
            var_ready = [sem(tag + f"var{n}_ready") for n in range(3)]
            rstd_ready = [sem(tag + f"rstd{n}_ready") for n in range(3)]
            h_ready = sem(tag + "h_ready")
            hi_ready = [sem(tag + f"hi{n}_ready") for n in range(2)]
            lo_ready = [sem(tag + f"lo{n}_ready") for n in range(2)]
            v0_ready = sem(tag + "v0_ready")
            p0_ready = [sem(tag + f"p0_half{n}_ready") for n in range(2)]
            x_used = sem(tag + "x_used")
            normed_ready = [sem(tag + f"normed{n}_ready") for n in range(2)]
            channels_ready = [sem(tag + f"channels{n}_ready") for n in range(3)]
            rv_next_ready = sem(tag + "rv_next_ready")
            rv_ready = sem(tag + "rv_ready")
            q_stacked = sem(tag + "q_stacked")
            k_stacked = sem(tag + "k_stacked")
            slot_filled = [sem(tag + "slot0_filled"), sem(tag + "slot1_filled")]
            p1_ready = sem(tag + "p1_ready")
            p1_summed = sem(tag + "p1_summed")
            values_done = sem(tag + "values_done")
            u_evicted = sem(tag + "u_evicted")
            den_filled = sem(tag + "den_filled")
            den_evicted = sem(tag + "den_evicted")
            u_tok_ready = sem(tag + "u_tok_ready")
            gate_arg_ready = sem(tag + "gate_arg_ready")
            gate_exp_ready = sem(tag + "gate_exp_ready")
            mixed_ready = sem(tag + "mixed_ready")
            result_ready = sem(tag + "result_ready")
            out_ready = sem(tag + "out_ready")
            if general:
                maxed = [sem(tag + f"maxed{n}") for n in range(2)]
                max_ready = [sem(tag + f"max{n}_ready") for n in range(2)]
                max_row_ready = [sem(tag + f"max_row{n}_ready") for n in range(2)]

            def sync_program(sp):
                def load(b):
                    sp.dma_start(x_sb[:, :], x_dram[bass.ds(b, 1), :, :].rearrange("b c n -> (b c) n"))\
                      .then_inc(x_loaded, 16)

                def load_next(b):
                    sp.wait_ge(x_used, halves * (b + 1))
                    load(b + 1)

                def store(b):
                    sp.wait_ge(out_ready, halves * (b + 1))
                    sp.dma_start(y_dram[bass.ds(b, 1), :, :].rearrange("b c n -> (b c) n"), out_sb[:, :])\
                      .then_inc(stored, 16)

                load(0)
                load_next(0)
                load_next(1)
                with sp.Fori(1, images - 2) as b:
                    store(b - 1)
                    load_next(b + 1)
                for b in range(images - 3, images):
                    store(b)
                sp.wait_ge(stored, 16 * (images + 1))

            def gpsimd_program(pool):
                def rstd(n):
                    def stage(b, arg):
                        width = 1 if n == 0 else tiles
                        into = moment0[:, 8:9] if n == 0 else moment1[:, 5, :]
                        of = moment0[:, 7:8] if n == 0 else moment1[:, 4, :]
                        pool.wait_ge(var_ready[n], b + 1)
                        pool.tensor_tensor(into, of, minus_half[:, 0:width], ALU.pow).then_inc(rstd_ready[n], 1)
                    return stage

                pool.memset(start_mark[:, :], 0.0).then_inc(stored, 16)
                in_order(pool, steps, images, lambda b, step: None,
                         {"norm_group_var": rstd(0), "ln1": rstd(1), "ln2": rstd(2)}, None, None, 0)

            def tensor_program(pe):
                banks = Banks()

                readers = [None, None]

                def open_bank(reader, value, awaited=None):
                    bank, _ = banks.take()
                    if readers[bank] and readers[bank][0] is not awaited:
                        pe.wait_ge(*readers[bank])
                    readers[bank] = (reader, value)
                    return ps_bank[:, bank, :], bank_filled[bank]

                def first_of_image(b):
                    last_reader = max_row_ready[1] if general else k_stacked
                    for half in range(halves):
                        readers[half] = (last_reader, halves * (PAIRS * b + 1) + half + 1)

                def group_mean_of(b, arg):
                    pe.wait_ge(moments_ready, b + 1)
                    out, filled = open_bank(mean_read, b + 1)
                    pe.matmul(out[:, 0:2], group_mean[:, :], moment0[:, 0:2], start=True, stop=True)\
                      .then_inc(filled, 1)

                def group_var_of(b, arg):
                    pe.wait_ge(spread_ready, b + 1)
                    out, filled = open_bank(var_ready[0], b + 1)
                    pe.matmul(out[:, 0:1], group_mean[:, :], moment0[:, 5:6], start=True, stop=True)\
                      .then_inc(filled, 1)

                def project(weight, source, ready, count, reader, per_image, order):
                    def stage(b, arg):
                        pe.wait_ge(ready, count * (b + 1))
                        for half in range(halves):
                            out, filled = open_bank(reader, per_image * b + order + half + 1, ready)
                            pe.matmul(out, weight, source[:, half * HALF:(half + 1) * HALF],
                                      start=True, stop=True).then_inc(filled, 1)
                    return stage

                def project_tokens(weight, source, ready, count, reader):
                    def stage(b, arg):
                        pe.wait_ge(ready, count * (b + 1))
                        for half in range(halves):
                            out, filled = open_bank(reader, halves * b + half + 1, ready)
                            for i in range(tiles_per_half):
                                at = half * HALF + i * P
                                last = pe.matmul(out[:, i * P:(i + 1) * P], source[:, at:at + P], weight,
                                                 start=True, stop=True)
                            last.then_inc(filled, 1)
                    return stage

                def turn(source, ready, count, reader):
                    def stage(b, arg):
                        pe.wait_ge(ready, count * (b + 1))
                        for half in range(halves):
                            out, filled = open_bank(reader, halves * b + half + 1, ready)
                            for i in range(tiles_per_half):
                                last = pe.transpose(out[:, i * P:(i + 1) * P],
                                                    source[:, half * tiles_per_half + i, :], ident[:, :])
                            last.then_inc(filled, 1)
                    return stage

                def max0(b, arg):
                    pe.wait_ge(hi_ready[0], 2 * halves * (b + 1))
                    pe.wait_ge(lo_ready[0], 2 * halves * (b + 1))
                    for i in range(tiles):
                        for half in range(halves):
                            out, filled = open_bank(maxed[0], halves * (tiles * b + i) + half + 1)
                            queries, keys = slice(i * P, (i + 1) * P), slice(half * HALF, (half + 1) * HALF)
                            pe.matmul(out, q_hi[:, queries], k_hi[:, keys], start=True, stop=False)
                            pe.matmul(out, q_hi[:, queries], k_lo[:, keys], start=False, stop=False)
                            pe.matmul(out, q_lo[:, queries], k_hi[:, keys], start=False, stop=True)\
                              .then_inc(filled, 1)
                    turn_maxima(0, b)

                def turn_maxima(layer, count):
                    pe.wait_ge(max_ready[layer], count + 1)
                    for half in range(halves):
                        out, filled = open_bank(max_row_ready[layer], halves * count + half + 1, max_ready[layer])
                        for i in range(tiles_per_half):
                            last = pe.transpose(out[:, i * P:(i + 1) * P],
                                                max_cols[:, half * tiles_per_half + i, :], ident[:, :])
                        last.then_inc(filled, 1)

                def score0(b, key_tile):
                    if key_tile == 0:
                        pe.wait_ge(hi_ready[0], 2 * halves * (b + 1))
                        pe.wait_ge(lo_ready[0], 2 * halves * (b + 1))
                        if general:
                            pe.wait_ge(max_row_ready[0], halves * (b + 1))
                    for half in range(halves):
                        out, filled = open_bank(p0_ready[half], tiles * b + key_tile + 1)
                        keys, queries = slice(key_tile * P, (key_tile + 1) * P), slice(half * HALF, (half + 1) * HALF)
                        pe.matmul(out, k_hi[:, keys], q_hi[:, queries], start=True, stop=False)
                        pe.matmul(out, k_hi[:, keys], q_lo[:, queries], start=False, stop=False)
                        if general:
                            pe.matmul(out, first_row[:, :], max_row[:, queries], start=False, stop=False)
                        pe.matmul(out, k_lo[:, keys], q_hi[:, queries], start=False, stop=True)\
                          .then_inc(filled, 1)

                def value0(b, query_tile):
                    if query_tile == 0:
                        pe.wait_ge(v0_ready, halves * (b + 1))
                        for half in range(halves):
                            pe.wait_ge(p0_ready[half], tiles * (b + 1))
                    out, filled = open_bank(value0_added, tiles * b + query_tile + 1)
                    for key_tile in range(tiles):
                        last = pe.matmul(out[:, 0:P + 1], p0[:, key_tile, query_tile * P:(query_tile + 1) * P],
                                         v0[:, key_tile, :], start=(key_tile == 0), stop=(key_tile == tiles - 1))
                    last.then_inc(filled, 1)

                def expand(b, pair):
                    pe.wait_ge(hi_ready[1], 2 * halves * (b + 1))
                    pe.wait_ge(lo_ready[1], 2 * halves * (b + 1))
                    for of_hi, of_lo, hi, lo, reader in ((q_of_hi, q_of_lo, q_hi, q_lo, q_stacked),
                                                         (k_of_hi, k_of_lo, k_hi, k_lo, k_stacked)):
                        for half in range(halves):
                            out, filled = open_bank(reader, halves * (PAIRS * b + pair) + half + 1)
                            at = slice(half * HALF, (half + 1) * HALF)
                            pe.matmul(out, of_hi[:, pair, :], hi[:, at], start=True, stop=False)
                            pe.matmul(out, of_lo[:, pair, :], lo[:, at], start=False, stop=True)\
                              .then_inc(filled, 1)

                def max1(b, pair):
                    pe.wait_ge(q_stacked, halves * (PAIRS * b + pair + 1))
                    pe.wait_ge(k_stacked, halves * (PAIRS * b + pair + 1))
                    awaited = k_stacked
                    for head in range(2 * pair, 2 * pair + 2):
                        for i in range(tiles):
                            for half in range(halves):
                                use = ((PAIRS * b + pair) * 2 + head % 2) * tiles + i
                                out, filled = open_bank(maxed[1], halves * use + half + 1, awaited)
                                pe.matmul(out, q_stack[:, pair, i * P:(i + 1) * P],
                                          k_stack[:, head, half * HALF:(half + 1) * HALF],
                                          start=True, stop=True).then_inc(filled, 1)
                    turn_maxima(1, PAIRS * b + pair)

                def attend(b, step):
                    phase, key_tile = divmod(step, tiles)
                    group, half = divmod(phase, halves)
                    queries, keys = slice(half * HALF, (half + 1) * HALF), slice(key_tile * P, (key_tile + 1) * P)
                    if step % (tiles * halves) == 0:
                        pairs_done = PAIRS * b + (group + 1) * GROUP // 2
                        pe.wait_ge(q_stacked, halves * pairs_done)
                        pe.wait_ge(k_stacked, halves * pairs_done)
                        if general:
                            pe.wait_ge(max_row_ready[1], halves * pairs_done)
                    for slot in range(2):
                        wait(pe, p1_ready, 2 * (steps_per_image * b + step - 1) + slot + 1)
                        for n in range(2):
                            head = GROUP * group + 2 * slot + n
                            last = pe.matmul(ps_score[:, slot, n, :], k_stack[:, head, keys],
                                             q_stack[:, head // 2, queries], start=True, stop=True)
                        last.then_inc(slot_filled[slot], 1)

                def sum_values(b, step):
                    phase, key_tile = divmod(step, tiles)
                    if step == 0:
                        pe.wait_ge(rv_ready, b + 1)
                    if key_tile == 0:
                        wait(pe, u_evicted, phases * b + phase)
                    for n in range(GROUP):
                        if n % 2 == 0:
                            pe.wait_ge(p1_ready, 2 * (steps_per_image * b + step) + n // 2 + 1)
                        last = pe.matmul(ps_u[n * QUAD:(n + 1) * QUAD, :], rv[:, key_tile, :],
                                         p1[:, step % ring, n, :], start=(key_tile == 0),
                                         stop=(key_tile == tiles - 1))
                    last.then_inc(values_done, 1)

                def den(b, phase):
                    pe.wait_ge(p1_summed, adds * (phases * b + phase + 1))
                    wait(pe, den_evicted, phases * b + phase)
                    for n in range(GROUP):
                        last = pe.matmul(ps_den[n * QUAD:(n + 1) * QUAD, :], ones[:, 0:QUAD], p_sum[:, n, :],
                                         start=True, stop=True)
                    last.then_inc(den_filled, 1)

                def retrieve_a(b, phase):
                    for source, ready, reader in ((u_sb, u_evicted, u_tok_ready), (den_sb, den_evicted, den_tok_ready)):
                        pe.wait_ge(ready, phases * b + phase + 1)
                        out, filled = open_bank(reader, phases * b + phase + 1)
                        for i in range(tiles_per_half):
                            last = pe.transpose(out[:, i * P:(i + 1) * P], source[:, i * P:(i + 1) * P], ident[:, :])
                        last.then_inc(filled, 1)

                stages = {
                    "norm_group_mean": group_mean_of, "norm_group_var": group_var_of,
                    "q0": project(qk_w[:, 0, :], work, h_ready, 1, lo_ready[0], 2 * halves, 0),
                    "k0": project(qk_w[:, 1, :], work, h_ready, 1, lo_ready[0], 2 * halves, halves),
                    "v0": project_tokens(value_w[:, :], work, h_ready, 1, v0_ready),
                    "max0": max0, "score0": score0,
                    "x_tokens": turn(x_sb[:, :].rearrange("c (i n) -> c i n", n=P), x_loaded, 16, x_used),
                    "value0": value0,
                    "ln1_channels": turn(work_tok, normed_ready[0], 1, channels_ready[0]),
                    "q1": project(wq_sb[:, :], channels, channels_ready[0], halves, lo_ready[1], 2 * halves, 0),
                    "k1": project(wk_sb[:, :], channels, channels_ready[0], halves, lo_ready[1], 2 * halves, halves),
                    "rv": project_tokens(wv_sb[:, :, :].rearrange("c a n -> c (a n)"), channels,
                                         channels_ready[0], halves, rv_next_ready),
                    "expand": expand, "max1": max1,
                    "rqk": project_tokens(gate_w[:, :], channels, channels_ready[0], halves, rqk_ready),
                    "den": den, "retrieve_a": retrieve_a,
                    "mixed_channels": turn(mixed, mixed_ready, phases, channels_ready[1]),
                    "out1": project_tokens(w_out_sb[:, :], channels, channels_ready[1], halves, out1_added),
                    "ln2_channels": turn(work_tok, normed_ready[1], 1, channels_ready[2]),
                    "ffn": project_tokens(ffn_w_sb[:, :], channels, channels_ready[2], halves, result_ready),
                    "result": turn(t_core, result_ready, halves, out_ready),
                }
                in_order(pe, steps, images, attend, stages, banks, None, 0, first_of_image, sum_values)

            def scalar_program(act):
                banks = Banks()

                def read_bank():
                    bank, before = banks.take()
                    act.wait_ge(bank_filled[bank], before + 1)
                    return ps_bank[:, bank, :]

                def halves_to(of_half, ready):
                    def stage(b, arg):
                        for half in range(halves):
                            bank = read_bank()
                            to, columns = of_half(half)
                            act.copy(to, columns(bank)).then_inc(ready, 1)
                    return stage

                def upper_part(to, layer):
                    def stage(b, arg):
                        for half in range(halves):
                            bank = read_bank()
                            at = slice(half * HALF, (half + 1) * HALF)
                            bias = 0.0 if layer else qkv_bias[:, (0 if to is q_hi else 1):(1 if to is q_hi else 2)]
                            act.activation(to[:, at], bank, ACT.Identity, bias=bias)\
                               .then_inc(hi_ready[layer], 1)
                    return stage

                def v0_part(half):
                    return (v0[:, half * tiles_per_half:(half + 1) * tiles_per_half, 0:P],
                            lambda bank: bank.rearrange("p (i c) -> p i c", c=P))

                def channels_part(half):
                    return channels[:, half * HALF:(half + 1) * HALF], lambda bank: bank

                def rv_part(half):
                    return (rv_next[:, half * tiles_per_half:(half + 1) * tiles_per_half, :],
                            lambda bank: bank.rearrange("p (i c) -> p i c", c=P)[:, :, 0:QUAD])

                def score0(b, key_tile):
                    for half in range(halves):
                        bank = read_bank()
                        act.activation(p0[:, key_tile, half * HALF:(half + 1) * HALF], bank, ACT.Exp, scale=scale0)\
                           .then_inc(p0_ready[half], 1)

                def skip_then(n, stage):
                    def both(b, arg):
                        for _ in range(n):
                            banks.take()
                        stage(b, arg)
                    return both

                def max_row0(b, arg):
                    for half in range(halves):
                        bank = read_bank()
                        act.copy(max_row[:, half * HALF:(half + 1) * HALF], bank)\
                           .then_inc(max_row_ready[0], 1)

                def max_row1(b, pair):
                    for half in range(halves):
                        bank = read_bank()
                        act.copy(q_stack[3 * QUAD:, pair, half * HALF:(half + 1) * HALF], bank[3 * QUAD:, :])\
                           .then_inc(max_row_ready[1], 1)

                def expand(b, pair):
                    for half in range(halves):
                        bank = read_bank()
                        act.copy(q_stack[:, pair, half * HALF:(half + 1) * HALF], bank)\
                           .then_inc(q_stacked, 1)
                    banks.taken += halves

                def take_values(b, arg):
                    act.wait_ge(rv_next_ready, halves * (b + 1))
                    wait(act, values_done, steps_per_image * b)
                    act.copy(rv[:, :, :], rv_next[:, :, :]).then_inc(rv_ready, 1)

                def attend(b, step):
                    done = steps_per_image * b + step
                    wait(act, values_done, done - ring + 1)
                    phase, key_tile = divmod(step - ring, tiles)
                    wait(act, p1_summed, adds * (phases * b + phase) + max(key_tile, 1))
                    for slot in range(2):
                        act.wait_ge(slot_filled[slot], done + 1)
                        act.activation(p1[:, step % ring, 2 * slot:2 * slot + 2, :], ps_score[:, slot, :, :],
                                       ACT.Exp, scale=scale1).then_inc(p1_ready, 1)

                def evict_u(b, phase):
                    act.wait_ge(values_done, tiles * (phases * b + phase + 1))
                    act.copy(u_sb[:, :], ps_u[:, :]).then_inc(u_evicted, 1)

                def retrieve_a(b, phase):
                    bank = read_bank()
                    wait(act, mixed_ready, phases * b + phase)
                    act.copy(u_tok[:, :, :, :].rearrange("p i h r -> p (i h r)"), bank)\
                       .then_inc(u_tok_ready, 1)
                    banks.take()

                def retrieve_b(b, phase):
                    act.wait_ge(gate_arg_ready, phases * b + phase + 1)
                    act.activation(small[:, 3, :], small[:, 2, :], ACT.Exp).then_inc(gate_exp_ready, 1)

                def result(b, arg):
                    act.wait_ge(stored, 16 * (b + 1))
                    for half in range(halves):
                        bank = read_bank()
                        act.copy(out_sb[:, half * HALF:(half + 1) * HALF], bank)\
                           .then_inc(out_ready, 1)

                stages = {
                    "q0": upper_part(q_hi, 0), "k0": upper_part(k_hi, 0),
                    "v0": halves_to(v0_part, v0_ready), "score0": score0,
                    "ln1_channels": halves_to(channels_part, channels_ready[0]),
                    "q1": upper_part(q_hi, 1), "k1": upper_part(k_hi, 1),
                    "rv": halves_to(rv_part, rv_next_ready),
                    "expand": expand, "take_values": take_values,
                    "evict_u": evict_u, "retrieve_a": retrieve_a, "retrieve_b": retrieve_b,
                    "mixed_channels": halves_to(channels_part, channels_ready[1]),
                    "ln2_channels": halves_to(channels_part, channels_ready[2]), "result": result,
                }
                if general:
                    stages["max0"] = skip_then(tiles * halves, max_row0)
                    stages["max1"] = skip_then(2 * tiles * halves, max_row1)
                in_order(act, steps, images, attend, stages, banks, None, 0)

            def vector_program(dve):
                banks, links = Banks(), Links(dve_link)

                def link(instruction):
                    instruction.then_inc(links.sem, 1)
                    dve.wait_ge(links.sem, links.next())

                def read_bank():
                    bank, before = banks.take()
                    dve.wait_ge(bank_filled[bank], before + 1)
                    return ps_bank[:, bank, :]

                m0 = moment0

                def norm_group_mean(b, arg):
                    dve.wait_ge(x_loaded, 16 * (b + 1))
                    for half in range(halves):
                        last = dve.bn_stats(stat0[:, half, :], x_sb[:, half * HALF:(half + 1) * HALF])
                    link(last)
                    means, spreads = stat0[:, :, 1:6:3], stat0[:, :, 2:6:3]
                    dve.tensor_reduce(m0[:, 2:3], spreads, AXIS.XY, ALU.add)
                    link(dve.tensor_reduce(m0[:, 3:4], means, AXIS.XY, ALU.add))
                    parts = 2 * halves
                    link(dve.tensor_scalar(m0[:, 0:1], m0[:, 3:4], 1.0 / parts, None, ALU.mult))
                    dev = part_dev[:, :].rearrange("p (a b) -> p a b", a=halves)
                    link(dve.tensor_scalar(dev, means, m0[:, 0:1], None, ALU.subtract))
                    link(dve.tensor_tensor(dev, dev, dev, ALU.mult))
                    link(dve.tensor_reduce(m0[:, 4:5], part_dev[:, :], AXIS.X, ALU.add))
                    link(dve.tensor_scalar(m0[:, 4:5], m0[:, 4:5], 1.0 / parts, None, ALU.mult))
                    dve.scalar_tensor_tensor(out=m0[:, 1:2], in0=m0[:, 2:3], scalar=1.0 / tokens, in1=m0[:, 4:5],
                                             op0=ALU.mult, op1=ALU.add).then_inc(moments_ready, 1)
                    bank = read_bank()
                    dve.tensor_copy(m0[:, 9:11], bank[:, 0:2]).then_inc(mean_read, 1)
                    dve.wait_ge(mean_read, b + 1)
                    link(dve.tensor_tensor(m0[:, 11:12], m0[:, 0:1], m0[:, 9:10], ALU.subtract))
                    dve.tensor_tensor(m0[:, 5:6], m0[:, 11:12], m0[:, 11:12], ALU.mult).then_inc(spread_ready, 1)

                def norm_group_var(b, arg):
                    bank = read_bank()
                    dve.scalar_tensor_tensor(out=m0[:, 7:8], in0=bank[:, 0:1], scalar=EPS, in1=m0[:, 10:11],
                                             op0=ALU.add, op1=ALU.add).then_inc(var_ready[0], 1)

                def norm_apply(b, arg):
                    dve.wait_ge(rstd_ready[0], b + 1)
                    link(dve.tensor_tensor(m0[:, 6:7], m0[:, 8:9], norm_cols[:, 0:1], ALU.mult))
                    link(dve.tensor_tensor(m0[:, 11:12], m0[:, 9:10], m0[:, 6:7], ALU.mult))
                    link(dve.tensor_tensor(m0[:, 11:12], norm_cols[:, 1:2], m0[:, 11:12], ALU.subtract))
                    dve.tensor_scalar(work[:, :], x_sb[:, :], m0[:, 6:7], m0[:, 11:12], ALU.mult, ALU.add)\
                       .then_inc(h_ready, 1)

                def lower_part(hi, lo, layer):
                    def stage(b, arg):
                        order = 0 if hi is q_hi else halves
                        for half in range(halves):
                            bank = read_bank()
                            dve.wait_ge(hi_ready[layer], 2 * halves * b + order + half + 1)
                            at = slice(half * HALF, (half + 1) * HALF)
                            if layer:
                                last = dve.tensor_tensor(lo[:, at], bank, hi[:, at].bitcast(F32), ALU.subtract)
                            else:
                                bias = qkv_bias[:, 0:1] if hi is q_hi else qkv_bias[:, 1:2]
                                last = dve.scalar_tensor_tensor(out=lo[:, at], in0=bank, scalar=bias,
                                                                in1=hi[:, at].bitcast(F32), op0=ALU.add,
                                                                op1=ALU.subtract)
                            last.then_inc(lo_ready[layer], 1)
                    return stage

                def max0(b, arg):
                    for i in range(tiles):
                        for half in range(halves):
                            bank = read_bank()
                            dve.tensor_reduce(max_part[:, 0, half, i:i + 1], bank, AXIS.X, ALU.max)\
                               .then_inc(maxed[0], 1)
                    dve.wait_ge(maxed[0], halves * tiles * (b + 1))
                    finish_max(1, 0, max_ready[0])
                    banks.taken += halves

                def max1(b, pair):
                    for n in range(2):
                        for i in range(tiles):
                            for half in range(halves):
                                bank = read_bank()
                                dve.tensor_reduce(max_part[:, n, half, i:i + 1], bank, AXIS.X, ALU.max)\
                                   .then_inc(maxed[1], 1)
                    dve.wait_ge(maxed[1], 2 * halves * tiles * (PAIRS * b + pair + 1))
                    finish_max(2, 3 * QUAD, max_ready[1])
                    banks.taken += halves

                def finish_max(count, column, ready):
                    link(dve.tensor_tensor(max_both[:, 0:count, :], max_part[:, 0:count, 0, :],
                                           max_part[:, 0:count, 1, :], ALU.max))
                    dve.tensor_scalar(max_cols[:, :, column:column + count],
                                      max_both[:, 0:count, :].rearrange("p n i -> p i n"), -1.0, None, ALU.mult)\
                       .then_inc(ready, 1)

                def x_tokens(b, arg):
                    for half in range(halves):
                        bank = read_bank()
                        at = slice(half * tiles_per_half, (half + 1) * tiles_per_half)
                        dve.tensor_tensor(t_front[:, at, :], bank.rearrange("p (i c) -> p i c", c=P),
                                          token_bias[:, :].unsqueeze(1).broadcast_to([P, tiles_per_half, P]),
                                          ALU.add).then_inc(x_used, 1)

                def value0(b, i):
                    if i == 0:
                        dve.wait_ge(x_used, halves * (b + 1))
                    bank = read_bank()
                    link(dve.reciprocal(den0[:, 1, i:i + 1], bank[:, P:P + 1]))
                    if not general:
                        dve.tensor_copy(den0[:, 0, i:i + 1], bank[:, P:P + 1])
                    last = dve.scalar_tensor_tensor(out=t_front[:, i, :], in0=bank[:, 0:P], scalar=den0[:, 1, i:i + 1],
                                                    in1=t_front[:, i, :], op0=ALU.mult, op1=ALU.add)
                    last.then_inc(value0_added, 1)
                    if i == tiles - 1:
                        dve.wait_ge(value0_added, tiles * (b + 1))
                        if not general:
                            watch(den0[:, 0, :], den0[:, 1, :], tiles)

                def watch(den, reciprocal, width):
                    dve.tensor_tensor(range_seen[:, 0, 0:width], range_seen[:, 0, 0:width], den, ALU.max)
                    dve.tensor_tensor(range_seen[:, 1, 0:width], range_seen[:, 1, 0:width], reciprocal, ALU.max)

                def layer_norm(n, source):
                    def stage(b, arg):
                        m1 = moment1
                        for i in range(tiles):
                            last = dve.bn_stats(stat1[:, i, :], source[:, i, :])
                        link(last)
                        dve.tensor_tensor(m1[:, 0, :], stat1[:, :, 1], stat1[:, :, 4], ALU.add)
                        dve.tensor_tensor(m1[:, 1, :], stat1[:, :, 1], stat1[:, :, 4], ALU.subtract)
                        link(dve.tensor_tensor(m1[:, 2, :], stat1[:, :, 2], stat1[:, :, 5], ALU.add))
                        link(dve.tensor_tensor(m1[:, 3, :], m1[:, 1, :], m1[:, 1, :], ALU.mult))
                        link(dve.tensor_scalar(m1[:, 2, :], m1[:, 2, :], 1.0 / P, EPS, ALU.mult, ALU.add))
                        dve.scalar_tensor_tensor(out=m1[:, 4, :], in0=m1[:, 3, :], scalar=0.25, in1=m1[:, 2, :],
                                                 op0=ALU.mult, op1=ALU.add).then_inc(var_ready[n + 1], 1)
                        dve.wait_ge(rstd_ready[n + 1], b + 1)
                        link(dve.scalar_tensor_tensor(out=m1[:, 6, :], in0=m1[:, 0, :], scalar=-0.5, in1=m1[:, 5, :],
                                                      op0=ALU.mult, op1=ALU.mult))
                        for i in range(tiles):
                            last = dve.tensor_scalar(work_tok[:, i, :], source[:, i, :], m1[:, 5, i:i + 1],
                                                     m1[:, 6, i:i + 1], ALU.mult, ALU.add)
                        last.then_inc(normed_ready[n], 1)
                    return stage

                def expand(b, pair):
                    banks.taken += halves
                    for half in range(halves):
                        bank = read_bank()
                        for n in range(2):
                            last = dve.tensor_scalar(k_stack[:, 2 * pair + n, half * HALF:(half + 1) * HALF], bank,
                                                     head_rows[:, n:n + 1], ident[:, 3 * QUAD + n:3 * QUAD + n + 1],
                                                     ALU.mult, ALU.add)
                        last.then_inc(k_stacked, 1)

                def rqk_tokens(b, arg):
                    for half in range(halves):
                        bank = read_bank()
                        at = slice(half * tiles_per_half, (half + 1) * tiles_per_half)
                        dve.tensor_copy(rqk[:, at, :], bank.rearrange("p (i c) -> p i c", c=P))\
                           .then_inc(rqk_ready, 1)
                    dve.wait_ge(rqk_ready, halves * (b + 1))

                def attend(b, step):
                    if step == 0:
                        if not isinstance(b, int) or b > 0:
                            add_weights(b - 1, steps_per_image - 1)
                    else:
                        add_weights(b, step - 1)
                    if isinstance(b, int) and b == images - 1 and step == steps_per_image - 1:
                        add_weights(b, step)

                def add_weights(b, step):
                    phase, key_tile = divmod(step, tiles)
                    if key_tile == 0:
                        return
                    dve.wait_ge(p1_ready, 2 * (steps_per_image * b + step) + 2)
                    if key_tile == 1:
                        wait(dve, den_filled, phases * b + phase)
                    else:
                        dve.wait_ge(p1_summed, adds * (phases * b + phase) + key_tile - 1)
                    before = p1[:, (step - 1) % ring, :, :] if key_tile == 1 else p_sum[:, :, :]
                    dve.tensor_tensor(p_sum[:, :, :], before, p1[:, step % ring, :, :], ALU.add)\
                       .then_inc(p1_summed, 1)

                def den(b, phase):
                    dve.wait_ge(den_filled, phases * b + phase + 1)
                    dve.tensor_copy(den_sb[:, :], ps_den[:, :]).then_inc(den_evicted, 1)

                def retrieve_a(b, phase):
                    group, half = divmod(phase, halves)
                    banks.take()
                    bank = read_bank()
                    den_rows = bank.rearrange("p (m r) -> p m r", r=QUAD)[:, :, 0]
                    dve.tensor_copy(den_tok[:, :], den_rows).then_inc(den_tok_ready, 1)
                    dve.wait_ge(den_tok_ready, phases * b + phase + 1)
                    link(dve.reciprocal(small[:, 0, :], den_tok[:, :]))
                    if not general:
                        watch(den_tok[:, :], small[:, 0, :], tiles_per_half * GROUP)
                    dve.wait_ge(u_tok_ready, phases * b + phase + 1)
                    keys = rqk[:, half * tiles_per_half:(half + 1) * tiles_per_half,
                               group * GROUP * HEAD_DIM:(group + 1) * GROUP * HEAD_DIM]
                    link(dve.tensor_tensor(prod[:, 0, :, :].rearrange("p (i h) d -> p i h d", h=GROUP),
                                           u_tok[:, :, :, HEAD_DIM:], keys.rearrange("p i (h d) -> p i h d", d=HEAD_DIM),
                                           ALU.mult))
                    link(dve.tensor_reduce(small[:, 1, :], prod[:, 0, :, :], AXIS.X, ALU.add))
                    link(dve.tensor_tensor(small[:, 1, :], small[:, 1, :], small[:, 0, :], ALU.mult))
                    dve.tensor_scalar(small[:, 2, :], small[:, 1, :], -scale1, EXP_ARG_MAX, ALU.mult, ALU.min)\
                       .then_inc(gate_arg_ready, 1)

                def retrieve_b(b, phase):
                    group, half = divmod(phase, halves)
                    dve.wait_ge(gate_exp_ready, phases * b + phase + 1)
                    link(dve.tensor_scalar(small[:, 4, :], small[:, 3, :], 1.0, None, ALU.add))
                    link(dve.reciprocal(small[:, 5, :], small[:, 4, :]))
                    link(dve.tensor_tensor(small[:, 5, :], small[:, 5, :], small[:, 0, :], ALU.mult))
                    flat = u_tok[:, :, :, :].rearrange("p i h r -> p (i h) r")
                    wide = [P, tiles_per_half * GROUP, HEAD_DIM]
                    dve.tensor_tensor(prod[:, 0, :, :], flat[:, :, 0:HEAD_DIM],
                                      small[:, 0, :].unsqueeze(2).broadcast_to(wide), ALU.mult)
                    link(dve.tensor_tensor(prod[:, 1, :, :], flat[:, :, HEAD_DIM:],
                                           small[:, 5, :].unsqueeze(2).broadcast_to(wide), ALU.mult))
                    if phase == 0:
                        wait(dve, channels_ready[1], halves * b)
                    to = mixed[:, half * tiles_per_half:(half + 1) * tiles_per_half,
                               group * GROUP * HEAD_DIM:(group + 1) * GROUP * HEAD_DIM]
                    dve.tensor_tensor(to.rearrange("p i (h d) -> p i h d", d=HEAD_DIM),
                                      prod[:, 0, :, :].rearrange("p (i h) d -> p i h d", h=GROUP),
                                      prod[:, 1, :, :].rearrange("p (i h) d -> p i h d", h=GROUP),
                                      ALU.add).then_inc(mixed_ready, 1)

                def add_bank(ready):
                    def stage(b, arg):
                        for half in range(halves):
                            bank = read_bank()
                            at = slice(half * tiles_per_half, (half + 1) * tiles_per_half)
                            dve.tensor_tensor(t_core[:, at, :], t_core[:, at, :],
                                              bank.rearrange("p (i c) -> p i c", c=P), ALU.add).then_inc(ready, 1)
                        dve.wait_ge(ready, halves * (b + 1))
                    return stage

                def take_tokens(b, arg):
                    wait(dve, out_ready, halves * b)
                    link(dve.tensor_copy(t_core[:, :, :], t_front[:, :, :]))

                stages = {
                    "norm_group_mean": norm_group_mean, "norm_group_var": norm_group_var, "norm_apply": norm_apply,
                    "q0": lower_part(q_hi, q_lo, 0), "k0": lower_part(k_hi, k_lo, 0),
                    "x_tokens": x_tokens, "value0": value0,
                    "ln1": layer_norm(0, t_front), "q1": lower_part(q_hi, q_lo, 1), "k1": lower_part(k_hi, k_lo, 1),
                    "expand": expand, "rqk": rqk_tokens, "den": den,
                    "retrieve_a": retrieve_a, "retrieve_b": retrieve_b, "out1": add_bank(out1_added),
                    "ln2": layer_norm(1, t_core), "ffn": add_bank(result_ready), "take_tokens": take_tokens,
                }
                if general:
                    stages.update(max0=max0, max1=max1)
                in_order(dve, steps, images, attend, stages, banks, links, links_per_image)

            with nc.Block() as block:
                @block.sync
                def _(sp):
                    sync_program(sp)

                @block.gpsimd
                def _(pool):
                    gpsimd_program(pool)

                @block.tensor
                def _(pe):
                    tensor_program(pe)

                @block.scalar
                def _(act):
                    scalar_program(act)

                @block.vector
                def _(dve):
                    vector_program(dve)

        one_pass(True)


_INS = ["x", "L0_conv_norm_w", "L0_conv_norm_b", "L0_conv_qkv_w", "L0_conv_qkv_b", "L0_conv_proj_w",
        "L0_conv_proj_b", "L1_attn_wq_s", "L1_attn_wk_s", "L1_attn_wv_r", "L1_attn_wq_r", "L1_attn_wk_ret",
        "L1_attn_w_out", "L1_ffn_qidx", "L1_ffn_scales", "L1_ffn_W"]


def kernel(**inputs):
    import concourse.bacc as bacc
    from concourse.bass_utils import run_bass_kernel_spmd

    nc = bacc.Bacc("TRN2", target_bir_lowering=False, num_devices=1)
    arrays, args = {}, []
    for name in _INS:
        a = np.ascontiguousarray(inputs[name])
        arrays[f"in_{name}"] = a
        args.append(nc.dram_tensor(f"in_{name}", a.shape, mybir.dt.from_np(a.dtype), kind="ExternalInput").ap())
    shape = inputs["x"].shape
    args.append(nc.dram_tensor("out_y", shape, F32, kind="ExternalOutput").ap())
    build(nc, *args)
    result = run_bass_kernel_spmd(nc, [arrays], core_ids=[0])
    return result.results[0]["out_y"]
```

```python
from contextlib import ExitStack

import numpy as np

import concourse.bass as bass
from concourse import mybir

F32 = mybir.dt.float32
F32R = mybir.dt.float32r
I32 = mybir.dt.int32
ALU = mybir.AluOpType
ACT = mybir.ActivationFunctionType
AXIS = mybir.AxisListType

P = 128
HALF = 512
HEADS = 8
HEAD_DIM = 16
RETRIEVERS = 2
PAIRS = HEADS // 2
GROUP = 4
QUAD = 32
GROUPS_L0 = 8
EPS = 1e-5
EXP_ARG_MAX = 80.0
NF4 = [-1.0, -0.6961928009986877, -0.5250730514526367, -0.39491748809814453, -0.28444138169288635,
       -0.18477343022823334, -0.09105003625154495, 0.0, 0.07958029955625534, 0.16093020141124725,
       0.24611230194568634, 0.33791524171829224, 0.44070982933044434, 0.5626170039176941,
       0.7229568362236023, 1.0]
NF4_BLOCK = 16

VECTOR_LINKS = 63
SCRATCH = 3
AHEAD = {"TAIL": -1, "HEAD": 0, "FRONT": 1, "NEXT": 2}


def banks_of(stage):
    return {
        "norm_group_mean": 1, "norm_group_var": 1, "q0": 2, "k0": 2, "v0": 2, "max0": 2, "max_rows0": 2,
        "score0": 1, "x_tokens": 2, "value0": 1, "ln1_channels": 2, "q1": 2, "k1": 2, "rv": 2,
        "max1": 1, "max_rows1": 1, "rqk": 2, "den": 1, "retrieve_a": 2, "mixed_channels": 2, "out1": 2,
        "ln2_channels": 2, "ffn": 2, "result": 2,
    }.get(stage, 0)


def schedule():
    steps = [[] for _ in range(32)]

    def put(step, image, stage, arg=0):
        steps[step].append((image, stage, arg))

    for phase in range(4):
        start = 8 * ((phase + 1) % 4)
        image = "HEAD" if phase < 3 else "TAIL"
        put(start, image, "evict_u", phase)
        put(start + 1, image, "den", phase)
        put(start + (2 if phase == 3 else 3), image, "retrieve_a", phase)
        put(start + (3 if phase == 3 else 4), image, "retrieve_b", phase)
    put(0, "HEAD", "take_values")
    put(3, "HEAD", "rqk")
    put(4, "TAIL", "mixed_channels")
    put(5, "TAIL", "out1")
    put(6, "TAIL", "ln2_stats")
    put(7, "TAIL", "ln2_apply")
    put(8, "TAIL", "ln2_channels")
    put(10, "TAIL", "ffn")
    put(12, "TAIL", "result")
    put(13, "HEAD", "take_tokens")
    for n, step in enumerate((29, 29, 30, 30, 31, 31, 0, 0, 8, 8, 10, 11, 11, 12, 12, 13)):
        put(step, "NEXT" if step > 16 else "FRONT", "score0", n)
    for n, step in enumerate((2, 4, 6, 7, 13, 14, 15, 16)):
        put(step, "FRONT", "value0", n)
    put(17, "FRONT", "ln1_stats")
    put(18, "FRONT", "ln1_apply")
    put(19, "FRONT", "ln1_channels")
    put(20, "FRONT", "q1")
    put(21, "FRONT", "k1")
    put(22, "FRONT", "hold_tokens")
    put(23, "FRONT", "rv")
    put(18, "NEXT", "norm_group_mean")
    put(19, "NEXT", "norm_group_var")
    put(20, "NEXT", "norm_apply")
    put(21, "NEXT", "q0")
    put(22, "NEXT", "k0")
    put(24, "NEXT", "v0")
    for n, step in enumerate((23, 23, 23, 24, 25, 26, 27, 27)):
        put(step, "NEXT", "max0", n)
    put(26, "NEXT", "x_tokens")
    put(28, "NEXT", "max_rows0")
    in_turn = []
    for step, others in enumerate(steps):
        ahead = (step // 8 + 1) % 4
        image = "HEAD" if ahead else "FRONT"
        n = step % 8
        if n == 7:
            others.insert(0, (image, "max_rows1", ahead))
        first, end = ((0, 5, 10, 15, 20, 24, 28, 32, 32)[n + d] for d in range(2))
        maxima = [(image, "max1", (ahead, use)) for use in range(first, end)]
        others = [("HEAD", "scores", (step, 0)), ("HEAD", "scores", (step, 1))] + others
        others.append(("HEAD", "values", step))
        merged, taken = [], 0
        for m, other in enumerate(others):
            merged.append(other)
            until = (m + 1) * len(maxima) // len(others)
            merged += maxima[taken:until]
            taken = until
        in_turn.append(merged)
    return in_turn


class Banks:

    def __init__(self):
        self.taken = 0
        self.looped = 0

    def take(self):
        bank, before = self.taken % SCRATCH, self.taken // SCRATCH + self.looped
        self.taken += 1
        return bank, before

    def skip(self, stage):
        self.taken += banks_of(stage)


class Links:

    def __init__(self, sem):
        self.sem = sem
        self.count = 0
        self.looped = 0

    def next(self):
        self.count += 1
        return self.count + self.looped


def wait(engine, sem, value):
    if not isinstance(value, int) or value > 0:
        engine.wait_ge(sem, value)


def in_order(engine, steps, images, stages, banks=None, links=None, first=None):

    def image_of(b, kinds):
        if first:
            first(b)
        for step in steps:
            for kind, stage, arg in step:
                if kind in kinds:
                    if stage in stages:
                        stages[stage](b + AHEAD[kind], arg)
                    elif banks:
                        banks.skip(stage)

    image_of(-2, ("NEXT",))
    image_of(-1, ("FRONT", "NEXT"))
    image_of(0, ("HEAD", "FRONT", "NEXT"))
    banks_per_image = sum(banks_of(stage) for step in steps for _, stage, _ in step)
    assert banks_per_image % SCRATCH == 0
    before = links.count if links else 0
    with engine.Fori(1, images - 2) as b:
        if banks:
            banks.looped = (b - 1) * (banks_per_image // SCRATCH)
        if links:
            links.looped = (b - 1) * VECTOR_LINKS
        image_of(b, tuple(AHEAD))
    if links:
        assert links.count - before == VECTOR_LINKS, links.count - before
        links.looped = (images - 4) * VECTOR_LINKS
    if banks:
        banks.looped = (images - 4) * (banks_per_image // SCRATCH)
    image_of(images - 2, ("HEAD", "TAIL", "FRONT"))
    image_of(images - 1, ("HEAD", "TAIL"))
    image_of(images, ("TAIL",))


def build(nc, x, norm_w, norm_b, qkv_w, qkv_b, proj_w, proj_b, wq_s, wk_s, wv_r, wq_r, wk_ret, w_out,
          qidx, scales, ffn_w, y):
    images, _, height, width = x.shape
    tokens = height * width
    tiles = tokens // P
    halves = tokens // HALF
    tiles_per_half = HALF // P
    scale0 = float(P) ** -0.5
    scale1 = float(HEAD_DIM) ** -0.5
    ring = 4
    phases = (HEADS // GROUP) * halves
    steps_per_image = phases * tiles
    adds = tiles - 2
    uses_per_phase = GROUP * tiles_per_half * halves
    stack_incs = 16 * 3 * 3 * (PAIRS // 2)
    x_dram = x.rearrange("b c h w -> b c (h w)")
    y_dram = y.rearrange("b c h w -> b c (h w)")

    with ExitStack() as ctx:
        def sb(name, shape, dtype=F32):
            return ctx.enter_context(nc.sbuf_tensor(name, shape, dtype))

        def psum(name, shape):
            return ctx.enter_context(nc.psum_tensor(name, shape, F32))

        def sem(name):
            return ctx.enter_context(nc.semaphore(name))

        ps_score = psum("ps_score", [P, 2, 2, HALF])
        ps_u = psum("ps_u", [P, HALF])
        ps_bank = psum("ps_bank", [P, SCRATCH, HALF])

        ident = sb("ident", [P, P])
        group_mean = sb("group_mean", [P, P])
        ones = sb("ones", [P, P])
        first_row = sb("first_row", [P, P], F32R)

        p0 = sb("p0", [P, tiles, HALF])
        setup_tiles = p0[:, :, :].rearrange("p a (b n) -> p (a b) n", n=P)
        qkv_rows = setup_tiles[:, 0:3, :]
        proj_rows, ffn_rows, wq_r_sb, wk_ret_blocks = (setup_tiles[:, n, :] for n in range(3, 7))
        bias_v, proj_bias, q_value, lora, lora_part = (setup_tiles[:, n, :] for n in range(7, 12))
        q_index = setup_tiles[:, 12, :].bitcast(I32)
        turned = setup_tiles[:, 13:17, :]
        qk_w = sb("qk_w", [P, 2, P])
        value_w = sb("value_w", [P, P])
        token_bias = sb("token_bias", [P, P])
        gate_w = sb("gate_w", [P, P])
        ffn_w_sb = sb("ffn_w_sb", [P, P])
        wq_sb = sb("wq_sb", [P, P])
        wk_sb = sb("wk_sb", [P, P])
        wv_r_sb = sb("wv_r_sb", [P, RETRIEVERS * HEAD_DIM])
        wv_sb = sb("wv_sb", [P, 4, QUAD])
        w_out_sb = sb("w_out_sb", [P, P])
        norm_cols = sb("norm_cols", [P, 2])
        qkv_bias = sb("qkv_bias", [P, 3])
        block_scale = sb("block_scale", [P, P // NF4_BLOCK])
        minus_half = sb("minus_half", [P, 8])

        x_sb = sb("x_sb", [P, tokens])
        stat0 = sb("stat0", [P, 2, 6])
        moment0 = sb("moment0", [P, 12])
        work = sb("work", [P, tokens])
        q_hi, q_lo, k_hi, k_lo = ([sb(f"{name}{layer}", [P, tokens], F32R) for layer in range(2)]
                                  for name in ("q_hi", "q_lo", "k_hi", "k_lo"))
        v0 = sb("v0", [P, tiles, P + 1])
        den0 = sb("den0", [P, tiles])
        t_front = sb("t_front", [P, tiles, P])
        t_held = sb("t_held", [P, tiles, P])
        t_core = sb("t_core", [P, tiles, P])

        stat1 = sb("stat1", [P, tiles, 6])
        moment1 = sb("moment1", [P, 8, tiles])
        channels = sb("channels", [P, tokens])
        q_stack = sb("q_stack", [P, PAIRS, tokens], F32R)
        k_stack = sb("k_stack", [P, HEADS, tokens], F32R)
        rv_next = sb("rv_next", [P, tiles, QUAD])
        rv = sb("rv", [P, tiles, QUAD])
        rqk = sb("rqk", [P, tiles, P])
        p1 = sb("p1", [P, ring, GROUP, HALF])
        p_sum = sb("p_sum", [P, GROUP, HALF])
        u_sb = sb("u_sb", [P, HALF])
        den_sb = sb("den_sb", [P, HALF])
        u_tok = sb("u_tok", [P, tiles_per_half, GROUP, QUAD])
        den_tok = sb("den_tok", [P, tiles_per_half * GROUP])
        small = sb("small", [P, 6, tiles_per_half * GROUP])
        prod = sb("prod", [P, 2, tiles_per_half * GROUP, HEAD_DIM])
        work_tok = work[:, :].rearrange("p (i c) -> p i c", c=P)
        start_mark = sb("start_mark", [P, 2])
        part_dev = sb("part_dev", [P, 2 * halves])
        max_part0 = sb("max_part0", [P, tiles, halves])
        max_cols0 = sb("max_cols0", [P, tiles, QUAD])
        max_row0 = sb("max_row0", [P, tokens], F32R)
        max_part1 = sb("max_part1", [P, tiles_per_half, GROUP, halves])
        max_cols1 = sb("max_cols1", [P, tiles_per_half, QUAD])
        mixed = sb("mixed", [P, tiles, P])
        out_sb = sb("out_sb", [P, tokens])

        weights_loaded = sem("weights_loaded")
        blocks_zeroed = sem("blocks_zeroed")
        pool_ready = sem("pool_ready")
        pool_link = sem("pool_link")
        turned_filled = sem("turned_filled")
        turned_ready = sem("turned_ready")
        folded_filled = sem("folded_filled")
        dve_setup = sem("dve_setup")
        weights_ready = sem("weights_ready")

        with nc.Block() as block:
            @block.sync
            def _(sp):
                loads = [
                    (qkv_rows, qkv_w.rearrange("(t o) c -> o t c", o=P)),
                    (proj_rows, proj_w), (ffn_rows, ffn_w), (wq_r_sb, wq_r),
                    (wq_sb[:, :], wq_s), (wk_sb[:, :], wk_s), (wv_r_sb[:, :], wv_r),
                    (w_out_sb[:, :], w_out), (q_index, qidx),
                    (block_scale[:, :], scales.rearrange("(o k) -> o k", o=P)),
                    (norm_cols[:, 0:1], norm_w.rearrange("(c a) -> c a", a=1)),
                    (norm_cols[:, 1:2], norm_b.rearrange("(c a) -> c a", a=1)),
                    (proj_bias, proj_b.partition_broadcast(P)),
                ]
                for to, source in loads:
                    sp.dma_start(to, source).then_inc(weights_loaded, 16)
                with nc.allow_non_contiguous_dma(reason="384 biases, once"):
                    sp.dma_start(qkv_bias[:, :], qkv_b.rearrange("(t o) -> o t", o=P)).then_inc(weights_loaded, 16)
                sp.wait_ge(blocks_zeroed, 1)
                for h in range(HEADS):
                    rows = slice(h * HEAD_DIM, (h + 1) * HEAD_DIM)
                    sp.dma_start(wk_ret_blocks[rows, rows], wk_ret).then_inc(weights_loaded, 16)

            @block.gpsimd
            def _(pool):
                links = Links(pool_link)

                def link(instruction):
                    instruction.then_inc(links.sem, 1)
                    pool.wait_ge(links.sem, links.next())

                pool.memset(wk_ret_blocks, 0.0).then_inc(blocks_zeroed, 1)
                pool.memset(minus_half[:, :], -0.5)
                pool.memset(ones[:, :], 1.0)
                link(pool.memset(ident[:, :], 0.0))
                link(pool.affine_select(out=ident[:, :], in_=ident[:, :], compare_op=ALU.not_equal, fill=1.0,
                                        base=0, pattern=[[-1, P]], channel_multiplier=1))
                size = P // GROUPS_L0
                blocks = group_mean[:, :].rearrange("p (g c) -> p g c", g=GROUPS_L0)
                link(pool.memset(group_mean[:, :], 1.0 / size))
                link(pool.affine_select(out=blocks, in_=blocks, compare_op=ALU.is_ge, fill=0.0, base=0,
                                        pattern=[[-size, GROUPS_L0], [0, size]], channel_multiplier=1))
                link(pool.affine_select(out=blocks, in_=blocks, compare_op=ALU.is_ge, fill=0.0, base=size - 1,
                                        pattern=[[size, GROUPS_L0], [0, size]], channel_multiplier=-1))
                pool.memset(v0[:, :, P:P + 1], 1.0).then_inc(pool_ready, 1)
                pool.wait_ge(weights_loaded, 16 * (14 + HEADS))
                link(pool.tensor_copy(q_value, q_index))
                link(pool.memset(lora, 0.0))
                for n, value in enumerate(NF4):
                    link(pool.tensor_scalar(lora_part, q_value, float(n), float(value),
                                            ALU.is_equal, ALU.mult))
                    link(pool.tensor_tensor(lora, lora, lora_part, ALU.add))
                pool.tensor_tensor(lora.rearrange("p (k j) -> p k j", j=NF4_BLOCK),
                                   lora.rearrange("p (k j) -> p k j", j=NF4_BLOCK),
                                   block_scale[:, :].unsqueeze(2).broadcast_to([P, P // NF4_BLOCK, NF4_BLOCK]),
                                   ALU.mult).then_inc(pool_ready, 1)

            @block.tensor
            def _(pe):
                scratch = ps_score[:, :, :, :].rearrange("p a b n -> p (a b n)")
                pe.wait_ge(pool_ready, 1)
                pe.wait_ge(weights_loaded, 16 * (14 + HEADS))
                for n, source in enumerate((qkv_rows[:, 0, :], qkv_rows[:, 1, :], proj_rows,
                                            ffn_rows, wq_r_sb, wk_ret_blocks)):
                    last = pe.transpose(scratch[:, n * P:(n + 1) * P], source, ident[:, :])
                last.then_inc(turned_filled, 1)
                pe.wait_ge(turned_ready, 1)
                pe.wait_ge(pool_ready, 2)
                for n, (left, right) in enumerate((
                        (qkv_rows[:, 2, :], turned[:, 0, :]),
                        (bias_v, turned[:, 0, :]),
                        (turned[:, 2, :], turned[:, 3, :]),
                        (lora, turned[:, 1, :]))):
                    last = pe.matmul(ps_bank[:, 0, n * P:(n + 1) * P], left, right, start=True, stop=True)
                last.then_inc(folded_filled, 1)

            @block.vector
            def _(dve):
                links = Links(dve_setup)

                def link(instruction):
                    instruction.then_inc(links.sem, 1)
                    dve.wait_ge(links.sem, links.next())

                dve.memset(max_cols0[:, :, :], 0.0)
                dve.memset(max_cols1[:, :, :], 0.0)
                dve.memset(max_row0[:, :].bitcast(F32), 0.0)
                dve.memset(q_stack[:, :, :].bitcast(F32), 0.0)
                link(dve.memset(k_stack[:, :, :].bitcast(F32), 0.0))
                dve.wait_ge(pool_ready, 1)
                dve.tensor_copy(first_row[:, :], ident[:, 0:1].broadcast_to([P, P]))
                for head in range(HEADS):
                    row = 3 * QUAD + head % GROUP
                    dve.tensor_copy(k_stack[3 * QUAD:, head, :],
                                    ident[3 * QUAD:, row:row + 1].broadcast_to([QUAD, tokens]))
                dve.wait_ge(weights_loaded, 16 * (14 + HEADS))
                dve.tensor_scalar(bias_v, ones[:, :], qkv_bias[:, 2:3], None, ALU.mult)
                for n in range(4):
                    dve.tensor_copy(wv_sb[:, n, 0:HEAD_DIM], wv_r_sb[:, HEAD_DIM:])
                    dve.tensor_tensor(wv_sb[:, n, HEAD_DIM:], wv_r_sb[:, 0:HEAD_DIM], wv_r_sb[:, HEAD_DIM:],
                                      ALU.subtract)
                dve.wait_ge(turned_filled, 1)
                scratch = ps_score[:, :, :, :].rearrange("p a b n -> p (a b n)")
                dve.tensor_copy(qk_w[:, :, :].rearrange("p a n -> p (a n)"), scratch[:, 0:2 * P])
                dve.tensor_copy(turned.rearrange("p a n -> p (a n)"), scratch[:, 2 * P:6 * P])\
                   .then_inc(turned_ready, 1)
                dve.wait_ge(folded_filled, 1)
                dve.tensor_copy(value_w[:, :], ps_bank[:, 0, 0:P])
                dve.tensor_tensor(token_bias[:, :], ps_bank[:, 0, P:2 * P], proj_bias, ALU.add)
                dve.tensor_copy(gate_w[:, :], ps_bank[:, 0, 2 * P:3 * P])
                dve.tensor_copy(ffn_w_sb[:, :], ps_bank[:, 0, 3 * P:4 * P]).then_inc(weights_ready, 1)

        def all_images():
            steps = schedule()

            x_loaded = sem("x_loaded")
            stored = sem("stored")
            bank_filled = [sem(f"bank{n}_filled") for n in range(SCRATCH)]
            mean_read = sem("mean_read")
            value0_added = sem("value0_added")
            rqk_ready = sem("rqk_ready")
            den_tok_ready = sem("den_tok_ready")
            out1_added = sem("out1_added")
            dve_link = sem("dve_link")
            moments_ready = sem("moments_ready")
            spread_ready = sem("spread_ready")
            var_ready = [sem(f"var{n}_ready") for n in range(3)]
            rstd_ready = [sem(f"rstd{n}_ready") for n in range(3)]
            h_ready = sem("h_ready")
            hi_ready = [sem(f"hi{n}_ready") for n in range(2)]
            lo_ready = [sem(f"lo{n}_ready") for n in range(2)]
            v0_ready = sem("v0_ready")
            p0_ready = sem("p0_ready")
            x_used = sem("x_used")
            normed_ready = [sem(f"normed{n}_ready") for n in range(2)]
            channels_ready = [sem(f"channels{n}_ready") for n in range(3)]
            rv_next_ready = sem("rv_next_ready")
            rv_ready = sem("rv_ready")
            slot_filled = [sem("slot0_filled"), sem("slot1_filled")]
            p1_ready = sem("p1_ready")
            p1_summed = sem("p1_summed")
            values_done = sem("values_done")
            u_evicted = sem("u_evicted")
            p_sum_used = sem("p_sum_used")
            den_evicted = sem("den_evicted")
            u_tok_ready = sem("u_tok_ready")
            gate_arg_ready = sem("gate_arg_ready")
            gate_exp_ready = sem("gate_exp_ready")
            mixed_ready = sem("mixed_ready")
            result_ready = sem("result_ready")
            out_ready = sem("out_ready")
            maxed = [sem(f"maxed{n}") for n in range(2)]
            max_ready = [sem(f"max{n}_ready") for n in range(2)]
            max_row_ready = [sem(f"max_row{n}_ready") for n in range(2)]
            stacked = [sem(f"stacked{n}") for n in range(2)]

            def sync_program(sp):
                def load(b):
                    wait(sp, x_used, halves * b)
                    sp.dma_start(x_sb[:, :], x_dram[bass.ds(b, 1), :, :].rearrange("b c n -> (b c) n"))\
                      .then_inc(x_loaded, 16)

                def stack(b, group):
                    sp.wait_ge(lo_ready[1], 2 * halves * (b + 1))
                    wait(sp, slot_filled[1], steps_per_image * (b - 1) + (group + 1) * steps_per_image // 2)
                    for pair in range(group * PAIRS // 2, (group + 1) * PAIRS // 2):
                        for part, (q_part, k_part) in enumerate(((q_hi, k_hi), (q_hi, k_lo), (q_lo, k_hi))):
                            sp.dma_start(q_stack[part * QUAD:(part + 1) * QUAD, pair, :].bitcast(F32),
                                         q_part[1][pair * QUAD:(pair + 1) * QUAD, :].bitcast(F32))\
                              .then_inc(stacked[group], 16)
                            for n in range(2):
                                at, row = pair * QUAD + n * HEAD_DIM, part * QUAD + n * HEAD_DIM
                                sp.dma_start(k_stack[row:row + HEAD_DIM, 2 * pair + n, :].bitcast(F32),
                                             k_part[1][at:at + HEAD_DIM, :].bitcast(F32))\
                                  .then_inc(stacked[group], 16)

                def store(b):
                    sp.wait_ge(out_ready, halves * (b + 1))
                    sp.dma_start(y_dram[bass.ds(b, 1), :, :].rearrange("b c n -> (b c) n"), out_sb[:, :])\
                      .then_inc(stored, 16)

                load(0)
                load(1)
                stack(0, 0)
                stack(0, 1)
                load(2)
                stack(1, 0)
                load(3)
                with sp.Fori(1, images - 3) as b:
                    stack(b, 1)
                    store(b - 1)
                    stack(b + 1, 0)
                    load(b + 3)
                stack(images - 3, 1)
                store(images - 4)
                stack(images - 2, 0)
                stack(images - 2, 1)
                store(images - 3)
                stack(images - 1, 0)
                stack(images - 1, 1)
                store(images - 2)
                store(images - 1)
                sp.wait_ge(stored, 16 * (images + 1))

            def gpsimd_program(pool):
                def rstd(n):
                    def stage(b, arg):
                        width = 1 if n == 0 else tiles
                        into = moment0[:, 8:9] if n == 0 else moment1[:, 5, :]
                        of = moment0[:, 7:8] if n == 0 else moment1[:, 4, :]
                        pool.wait_ge(var_ready[n], b + 1)
                        pool.tensor_tensor(into, of, minus_half[:, 0:width], ALU.pow).then_inc(rstd_ready[n], 1)
                    return stage

                pool.memset(start_mark[:, :], 0.0).then_inc(stored, 16)

                def add_weights(b, step):
                    phase, key_tile = divmod(step, tiles)
                    if not 1 <= key_tile <= adds:
                        return
                    pool.wait_ge(p1_ready, 2 * (steps_per_image * b + step) + 2)
                    if key_tile == 1:
                        wait(pool, p_sum_used, phases * b + phase)
                    else:
                        pool.wait_ge(p1_summed, adds * (phases * b + phase) + key_tile - 1)
                    before = p1[:, (step - 1) % ring, :, :] if key_tile == 1 else p_sum[:, :, :]
                    pool.tensor_tensor(p_sum[:, :, :], before, p1[:, step % ring, :, :], ALU.add)\
                        .then_inc(p1_summed, 1)

                in_order(pool, steps, images, {"values": add_weights, "norm_group_var": rstd(0),
                                               "ln1_stats": rstd(1), "ln2_stats": rstd(2)})

            def tensor_program(pe):
                banks = Banks()

                readers = []
                first_readers = []

                def open_bank(reader, value, awaited=None):
                    bank, _ = banks.take()
                    if len(readers) >= SCRATCH and readers[-SCRATCH][0] is not awaited:
                        pe.wait_ge(*readers[-SCRATCH])
                    readers.append((reader, value))
                    return ps_bank[:, bank, :], bank_filled[bank]

                def first_of_image(b):
                    if isinstance(b, int) and b < images - 2:
                        first_readers.append(readers[-SCRATCH:])
                    elif not isinstance(b, int) or b == images - 2:
                        if not isinstance(b, int):
                            first_readers.append(readers[-SCRATCH:])
                        for (reader, value0), (_, value1) in zip(*first_readers[-2:]):
                            readers.append((reader, value1 + (b - 1) * (value1 - value0)))

                def group_mean_of(b, arg):
                    pe.wait_ge(moments_ready, b + 1)
                    out, filled = open_bank(mean_read, b + 1)
                    pe.matmul(out[:, 0:2], group_mean[:, :], moment0[:, 0:2], start=True, stop=True)\
                      .then_inc(filled, 1)

                def group_var_of(b, arg):
                    pe.wait_ge(spread_ready, b + 1)
                    out, filled = open_bank(var_ready[0], b + 1)
                    pe.matmul(out[:, 0:1], group_mean[:, :], moment0[:, 5:6], start=True, stop=True)\
                      .then_inc(filled, 1)

                def project(weight, source, ready, count, reader, per_image, order):
                    def stage(b, arg):
                        pe.wait_ge(ready, count * (b + 1))
                        for half in range(halves):
                            out, filled = open_bank(reader, per_image * b + order + half + 1, ready)
                            pe.matmul(out, weight, source[:, half * HALF:(half + 1) * HALF],
                                      start=True, stop=True).then_inc(filled, 1)
                    return stage

                def project_tokens(weight, source, ready, count, reader):
                    def stage(b, arg):
                        pe.wait_ge(ready, count * (b + 1))
                        for half in range(halves):
                            out, filled = open_bank(reader, halves * b + half + 1, ready)
                            for i in range(tiles_per_half):
                                at = half * HALF + i * P
                                last = pe.matmul(out[:, i * P:(i + 1) * P], source[:, at:at + P], weight,
                                                 start=True, stop=True)
                            last.then_inc(filled, 1)
                    return stage

                def turn(source, ready, count, reader):
                    def stage(b, arg):
                        pe.wait_ge(ready, count * (b + 1))
                        for half in range(halves):
                            out, filled = open_bank(reader, halves * b + half + 1, ready)
                            for i in range(tiles_per_half):
                                last = pe.transpose(out[:, i * P:(i + 1) * P],
                                                    source[:, half * tiles_per_half + i, :], ident[:, :])
                            last.then_inc(filled, 1)
                    return stage

                def max0(b, i):
                    if i == 0:
                        pe.wait_ge(lo_ready[0], 2 * halves * (b + 1))
                    for half in range(halves):
                        out, filled = open_bank(maxed[0], halves * (tiles * b + i) + half + 1,
                                                lo_ready[0] if i == 0 else None)
                        pe.matmul(out, q_hi[0][:, i * P:(i + 1) * P], k_hi[0][:, half * HALF:(half + 1) * HALF],
                                  start=True, stop=True).then_inc(filled, 1)

                def max_rows0(b, arg):
                    pe.wait_ge(max_ready[0], b + 1)
                    for half in range(halves):
                        out, filled = open_bank(max_row_ready[0], halves * b + half + 1)
                        for i in range(tiles_per_half):
                            last = pe.transpose(out[0:QUAD, i * P:(i + 1) * P],
                                                max_cols0[:, half * tiles_per_half + i, :], ident[:, :])
                        last.then_inc(filled, 1)

                def score0(b, n):
                    half, key_tile = divmod(n, tiles)
                    if n == 0:
                        pe.wait_ge(max_row_ready[0], halves * (b + 1))
                    out, filled = open_bank(p0_ready, halves * tiles * b + n + 1, max_row_ready[0] if n == 0 else None)
                    keys, queries = slice(key_tile * P, (key_tile + 1) * P), slice(half * HALF, (half + 1) * HALF)
                    pe.matmul(out, k_hi[0][:, keys], q_hi[0][:, queries], start=True, stop=False)
                    pe.matmul(out, k_hi[0][:, keys], q_lo[0][:, queries], start=False, stop=False)
                    pe.matmul(out, first_row[:, :], max_row0[:, queries], start=False, stop=False)
                    pe.matmul(out, k_lo[0][:, keys], q_hi[0][:, queries], start=False, stop=True).then_inc(filled, 1)

                def value0(b, query_tile):
                    awaited = None
                    if query_tile % tiles_per_half == 0:
                        half = query_tile // tiles_per_half
                        pe.wait_ge(v0_ready, halves * (b + 1))
                        pe.wait_ge(p0_ready, tiles * (halves * b + half + 1))
                        awaited = p0_ready
                    out, filled = open_bank(value0_added, tiles * b + query_tile + 1, awaited)
                    at = query_tile % tiles_per_half * P
                    for key_tile in range(tiles):
                        last = pe.matmul(out[:, 0:P + 1], p0[:, key_tile, at:at + P], v0[:, key_tile, :],
                                         start=(key_tile == 0), stop=(key_tile == tiles - 1))
                    last.then_inc(filled, 1)

                def max1(b, arg):
                    phase, use = arg
                    group, q_half = divmod(phase, halves)
                    if use == 0:
                        pe.wait_ge(stacked[group], stack_incs * (b + 1))
                    i, n, half = use // (GROUP * halves), use // halves % GROUP, use % halves
                    head, at = group * GROUP + n, (q_half * tiles_per_half + i) * P
                    out, filled = open_bank(maxed[1], uses_per_phase * (phases * b + phase) + use + 1)
                    pe.matmul(out, q_stack[0:3 * QUAD, head // 2, at:at + P],
                              k_stack[0:3 * QUAD, head, half * HALF:(half + 1) * HALF],
                              start=True, stop=True).then_inc(filled, 1)

                def max_rows1(b, phase):
                    pe.wait_ge(max_ready[1], phases * b + phase + 1)
                    out, filled = open_bank(max_row_ready[1], phases * b + phase + 1)
                    for i in range(tiles_per_half):
                        last = pe.transpose(out[0:QUAD, i * P:(i + 1) * P], max_cols1[:, i, :], ident[:, :])
                    last.then_inc(filled, 1)

                def scores(b, arg):
                    step, slot = arg
                    phase, key_tile = divmod(step, tiles)
                    group, half = divmod(phase, halves)
                    queries, keys = slice(half * HALF, (half + 1) * HALF), slice(key_tile * P, (key_tile + 1) * P)
                    if key_tile == 0 and slot == 0:
                        pe.wait_ge(max_row_ready[1], phases * b + phase + 1)
                    wait(pe, p1_ready, 2 * (steps_per_image * b + step - 1) + slot + 1)
                    for n in range(2):
                        head = GROUP * group + 2 * slot + n
                        last = pe.matmul(ps_score[:, slot, n, :], k_stack[:, head, keys],
                                         q_stack[:, head // 2, queries], start=True, stop=True)
                    last.then_inc(slot_filled[slot], 1)

                def sum_values(b, step):
                    phase, key_tile = divmod(step, tiles)
                    if step == 0:
                        pe.wait_ge(rv_ready, b + 1)
                    if key_tile == 0:
                        wait(pe, u_evicted, phases * b + phase)
                    for n in range(GROUP):
                        if n % 2 == 0:
                            pe.wait_ge(p1_ready, 2 * (steps_per_image * b + step) + n // 2 + 1)
                        last = pe.matmul(ps_u[n * QUAD:(n + 1) * QUAD, :], rv[:, key_tile, :],
                                         p1[:, step % ring, n, :], start=(key_tile == 0),
                                         stop=(key_tile == tiles - 1))
                    last.then_inc(values_done, 1)

                def den(b, phase):
                    pe.wait_ge(p1_summed, adds * (phases * b + phase + 1))
                    out, filled = open_bank(den_evicted, phases * b + phase + 1)
                    last_weights = p1[:, (phase * tiles + tiles - 1) % ring, :, :]
                    for source in (p_sum, last_weights):
                        for n in range(GROUP):
                            last = pe.matmul(out[n * QUAD:(n + 1) * QUAD, :], ones[:, 0:QUAD], source[:, n, :],
                                             start=(source is p_sum), stop=(source is last_weights))
                        last.then_inc(p_sum_used if source is p_sum else filled, 1)

                def retrieve_a(b, phase):
                    for source, ready, reader in ((u_sb, u_evicted, u_tok_ready), (den_sb, den_evicted, den_tok_ready)):
                        pe.wait_ge(ready, phases * b + phase + 1)
                        out, filled = open_bank(reader, phases * b + phase + 1, ready)
                        for i in range(tiles_per_half):
                            last = pe.transpose(out[:, i * P:(i + 1) * P], source[:, i * P:(i + 1) * P], ident[:, :])
                        last.then_inc(filled, 1)

                stages = {
                    "norm_group_mean": group_mean_of, "norm_group_var": group_var_of,
                    "q0": project(qk_w[:, 0, :], work, h_ready, 1, lo_ready[0], 2 * halves, 0),
                    "k0": project(qk_w[:, 1, :], work, h_ready, 1, lo_ready[0], 2 * halves, halves),
                    "v0": project_tokens(value_w[:, :], work, h_ready, 1, v0_ready),
                    "max0": max0, "max_rows0": max_rows0, "score0": score0,
                    "x_tokens": turn(x_sb[:, :].rearrange("c (i n) -> c i n", n=P), x_loaded, 16, x_used),
                    "value0": value0,
                    "ln1_channels": turn(work_tok, normed_ready[0], 1, channels_ready[0]),
                    "q1": project(wq_sb[:, :], channels, channels_ready[0], halves, lo_ready[1], 2 * halves, 0),
                    "k1": project(wk_sb[:, :], channels, channels_ready[0], halves, lo_ready[1], 2 * halves, halves),
                    "rv": project_tokens(wv_sb[:, :, :].rearrange("c a n -> c (a n)"), channels,
                                         channels_ready[0], halves, rv_next_ready),
                    "max1": max1, "max_rows1": max_rows1,
                    "rqk": project_tokens(gate_w[:, :], channels, channels_ready[0], halves, rqk_ready),
                    "scores": scores, "values": sum_values, "den": den, "retrieve_a": retrieve_a,
                    "mixed_channels": turn(mixed, mixed_ready, phases, channels_ready[1]),
                    "out1": project_tokens(w_out_sb[:, :], channels, channels_ready[1], halves, out1_added),
                    "ln2_channels": turn(work_tok, normed_ready[1], 1, channels_ready[2]),
                    "ffn": project_tokens(ffn_w_sb[:, :], channels, channels_ready[2], halves, result_ready),
                    "result": turn(t_core, result_ready, halves, out_ready),
                }
                in_order(pe, steps, images, stages, banks, first=first_of_image)

            def scalar_program(act):
                banks = Banks()

                def read_bank():
                    bank, before = banks.take()
                    act.wait_ge(bank_filled[bank], before + 1)
                    return ps_bank[:, bank, :]

                def halves_to(of_half, ready):
                    def stage(b, arg):
                        for half in range(halves):
                            bank = read_bank()
                            to, columns = of_half(half)
                            act.copy(to, columns(bank)).then_inc(ready, 1)
                    return stage

                def upper_part(to, layer):
                    def stage(b, arg):
                        if layer:
                            for group in range(2):
                                wait(act, stacked[group], stack_incs * b)
                        for half in range(halves):
                            bank = read_bank()
                            at = slice(half * HALF, (half + 1) * HALF)
                            bias = 0.0 if layer else qkv_bias[:, (0 if to is q_hi[0] else 1):(1 if to is q_hi[0] else 2)]
                            act.activation(to[:, at], bank, ACT.Identity, bias=bias)\
                               .then_inc(hi_ready[layer], 1)
                    return stage

                def v0_part(half):
                    return (v0[:, half * tiles_per_half:(half + 1) * tiles_per_half, 0:P],
                            lambda bank: bank.rearrange("p (i c) -> p i c", c=P))

                def channels_part(half):
                    return channels[:, half * HALF:(half + 1) * HALF], lambda bank: bank

                def rv_part(half):
                    return (rv_next[:, half * tiles_per_half:(half + 1) * tiles_per_half, :],
                            lambda bank: bank.rearrange("p (i c) -> p i c", c=P)[:, :, 0:QUAD])

                def score0(b, n):
                    if n % tiles == 0:
                        wait(act, value0_added, tiles_per_half * (halves * b + n // tiles))
                    act.activation(p0[:, n % tiles, :], read_bank(), ACT.Exp, scale=scale0).then_inc(p0_ready, 1)

                def max_rows0(b, arg):
                    for half in range(halves):
                        act.copy(max_row0[0:QUAD, half * HALF:(half + 1) * HALF], read_bank()[0:QUAD, :])\
                           .then_inc(max_row_ready[0], 1)

                def max_rows1(b, phase):
                    group, half = divmod(phase, halves)
                    pairs = slice(group * GROUP // 2, (group + 1) * GROUP // 2)
                    act.copy(q_stack[3 * QUAD:, pairs, half * HALF:(half + 1) * HALF],
                             read_bank()[0:QUAD, :].unsqueeze(1).broadcast_to([QUAD, GROUP // 2, HALF]))\
                       .then_inc(max_row_ready[1], 1)

                def take_values(b, arg):
                    act.wait_ge(rv_next_ready, halves * (b + 1))
                    wait(act, values_done, steps_per_image * b)
                    act.copy(rv[:, :, :], rv_next[:, :, :]).then_inc(rv_ready, 1)

                def weights(b, arg):
                    step, slot = arg
                    done = steps_per_image * b + step
                    if slot == 0:
                        wait(act, values_done, done - ring + 1)
                        phase, key_tile = divmod(step - ring, tiles)
                        if key_tile <= adds:
                            wait(act, p1_summed, adds * (phases * b + phase) + max(key_tile, 1))
                        else:
                            wait(act, den_evicted, phases * b + phase + 1)
                    act.wait_ge(slot_filled[slot], done + 1)
                    act.activation(p1[:, step % ring, 2 * slot:2 * slot + 2, :], ps_score[:, slot, :, :],
                                   ACT.Exp, scale=scale1).then_inc(p1_ready, 1)

                def evict_u(b, phase):
                    act.wait_ge(values_done, tiles * (phases * b + phase + 1))
                    act.copy(u_sb[:, :], ps_u[:, :]).then_inc(u_evicted, 1)

                def retrieve_a(b, phase):
                    bank = read_bank()
                    wait(act, mixed_ready, phases * b + phase)
                    act.copy(u_tok[:, :, :, :].rearrange("p i h r -> p (i h r)"), bank)\
                       .then_inc(u_tok_ready, 1)
                    banks.take()

                def retrieve_b(b, phase):
                    act.wait_ge(gate_arg_ready, phases * b + phase + 1)
                    act.activation(small[:, 3, :], small[:, 2, :], ACT.Exp).then_inc(gate_exp_ready, 1)

                def result(b, arg):
                    act.wait_ge(stored, 16 * (b + 1))
                    for half in range(halves):
                        bank = read_bank()
                        act.copy(out_sb[:, half * HALF:(half + 1) * HALF], bank)\
                           .then_inc(out_ready, 1)

                stages = {
                    "q0": upper_part(q_hi[0], 0), "k0": upper_part(k_hi[0], 0),
                    "v0": halves_to(v0_part, v0_ready), "score0": score0,
                    "ln1_channels": halves_to(channels_part, channels_ready[0]),
                    "q1": upper_part(q_hi[1], 1), "k1": upper_part(k_hi[1], 1),
                    "rv": halves_to(rv_part, rv_next_ready),
                    "max_rows0": max_rows0, "max_rows1": max_rows1, "take_values": take_values,
                    "scores": weights, "evict_u": evict_u, "retrieve_a": retrieve_a, "retrieve_b": retrieve_b,
                    "mixed_channels": halves_to(channels_part, channels_ready[1]),
                    "ln2_channels": halves_to(channels_part, channels_ready[2]), "result": result,
                }
                in_order(act, steps, images, stages, banks)

            def vector_program(dve):
                banks, links = Banks(), Links(dve_link)

                def link(instruction):
                    instruction.then_inc(links.sem, 1)
                    dve.wait_ge(links.sem, links.next())

                def read_bank():
                    bank, before = banks.take()
                    dve.wait_ge(bank_filled[bank], before + 1)
                    return ps_bank[:, bank, :]

                m0 = moment0

                def norm_group_mean(b, arg):
                    dve.wait_ge(x_loaded, 16 * (b + 1))
                    for half in range(halves):
                        last = dve.bn_stats(stat0[:, half, :], x_sb[:, half * HALF:(half + 1) * HALF])
                    link(last)
                    means, spreads = stat0[:, :, 1:6:3], stat0[:, :, 2:6:3]
                    dve.tensor_reduce(m0[:, 2:3], spreads, AXIS.XY, ALU.add)
                    link(dve.tensor_reduce(m0[:, 3:4], means, AXIS.XY, ALU.add))
                    parts = 2 * halves
                    link(dve.tensor_scalar(m0[:, 0:1], m0[:, 3:4], 1.0 / parts, None, ALU.mult))
                    dev = part_dev[:, :].rearrange("p (a b) -> p a b", a=halves)
                    link(dve.tensor_scalar(dev, means, m0[:, 0:1], None, ALU.subtract))
                    link(dve.tensor_tensor(dev, dev, dev, ALU.mult))
                    link(dve.tensor_reduce(m0[:, 4:5], part_dev[:, :], AXIS.X, ALU.add))
                    link(dve.tensor_scalar(m0[:, 4:5], m0[:, 4:5], 1.0 / parts, None, ALU.mult))
                    dve.scalar_tensor_tensor(out=m0[:, 1:2], in0=m0[:, 2:3], scalar=1.0 / tokens, in1=m0[:, 4:5],
                                             op0=ALU.mult, op1=ALU.add).then_inc(moments_ready, 1)
                    bank = read_bank()
                    dve.tensor_copy(m0[:, 9:11], bank[:, 0:2]).then_inc(mean_read, 1)
                    dve.wait_ge(mean_read, b + 1)
                    link(dve.tensor_tensor(m0[:, 11:12], m0[:, 0:1], m0[:, 9:10], ALU.subtract))
                    dve.tensor_tensor(m0[:, 5:6], m0[:, 11:12], m0[:, 11:12], ALU.mult).then_inc(spread_ready, 1)

                def norm_group_var(b, arg):
                    bank = read_bank()
                    dve.scalar_tensor_tensor(out=m0[:, 7:8], in0=bank[:, 0:1], scalar=EPS, in1=m0[:, 10:11],
                                             op0=ALU.add, op1=ALU.add).then_inc(var_ready[0], 1)

                def norm_apply(b, arg):
                    dve.wait_ge(rstd_ready[0], b + 1)
                    link(dve.tensor_tensor(m0[:, 6:7], m0[:, 8:9], norm_cols[:, 0:1], ALU.mult))
                    link(dve.tensor_tensor(m0[:, 11:12], m0[:, 9:10], m0[:, 6:7], ALU.mult))
                    link(dve.tensor_tensor(m0[:, 11:12], norm_cols[:, 1:2], m0[:, 11:12], ALU.subtract))
                    dve.tensor_scalar(work[:, :], x_sb[:, :], m0[:, 6:7], m0[:, 11:12], ALU.mult, ALU.add)\
                       .then_inc(h_ready, 1)

                def lower_part(hi, lo, layer):
                    def stage(b, arg):
                        order = 0 if hi is q_hi[layer] else halves
                        for half in range(halves):
                            bank = read_bank()
                            dve.wait_ge(hi_ready[layer], 2 * halves * b + order + half + 1)
                            at = slice(half * HALF, (half + 1) * HALF)
                            if layer:
                                last = dve.tensor_tensor(lo[:, at], bank, hi[:, at].bitcast(F32), ALU.subtract)
                            else:
                                bias = qkv_bias[:, 0:1] if hi is q_hi[0] else qkv_bias[:, 1:2]
                                last = dve.scalar_tensor_tensor(out=lo[:, at], in0=bank, scalar=bias,
                                                                in1=hi[:, at].bitcast(F32), op0=ALU.add,
                                                                op1=ALU.subtract)
                            last.then_inc(lo_ready[layer], 1)
                    return stage

                def max0(b, i):
                    for half in range(halves):
                        dve.tensor_reduce(max_part0[:, i, half:half + 1], read_bank(), AXIS.X, ALU.max)\
                           .then_inc(maxed[0], 1)
                    if i == tiles - 1:
                        dve.wait_ge(maxed[0], halves * tiles * (b + 1))
                        dve.tensor_reduce(max_cols0[:, :, 0], max_part0[:, :, :], AXIS.X, ALU.max, negate=True)\
                           .then_inc(max_ready[0], 1)

                def max1(b, arg):
                    phase, use = arg
                    i, n, half = use // (GROUP * halves), use // halves % GROUP, use % halves
                    dve.tensor_reduce(max_part1[:, i, n, half:half + 1], read_bank(), AXIS.X, ALU.max)\
                       .then_inc(maxed[1], 1)
                    if use == uses_per_phase - 1:
                        dve.wait_ge(maxed[1], uses_per_phase * (phases * b + phase + 1))
                        dve.tensor_reduce(max_cols1[:, :, 0:GROUP], max_part1[:, :, :, :], AXIS.X, ALU.max,
                                          negate=True).then_inc(max_ready[1], 1)

                def x_tokens(b, arg):
                    for half in range(halves):
                        bank = read_bank()
                        at = slice(half * tiles_per_half, (half + 1) * tiles_per_half)
                        dve.tensor_tensor(t_front[:, at, :], bank.rearrange("p (i c) -> p i c", c=P),
                                          token_bias[:, :].unsqueeze(1).broadcast_to([P, tiles_per_half, P]),
                                          ALU.add).then_inc(x_used, 1)

                def value0(b, i):
                    if i == 0:
                        dve.wait_ge(x_used, halves * (b + 1))
                    bank = read_bank()
                    link(dve.reciprocal(den0[:, i:i + 1], bank[:, P:P + 1]))
                    dve.scalar_tensor_tensor(out=t_front[:, i, :], in0=bank[:, 0:P], scalar=den0[:, i:i + 1],
                                             in1=t_front[:, i, :], op0=ALU.mult, op1=ALU.add)\
                       .then_inc(value0_added, 1)
                    if i == tiles - 1:
                        dve.wait_ge(value0_added, tiles * (b + 1))

                def layer_norm_stats(n, source):
                    def stage(b, arg):
                        m1 = moment1
                        for i in range(tiles):
                            last = dve.bn_stats(stat1[:, i, :], source[:, i, :])
                        link(last)
                        dve.tensor_tensor(m1[:, 0, :], stat1[:, :, 1], stat1[:, :, 4], ALU.add)
                        dve.tensor_tensor(m1[:, 1, :], stat1[:, :, 1], stat1[:, :, 4], ALU.subtract)
                        link(dve.tensor_tensor(m1[:, 2, :], stat1[:, :, 2], stat1[:, :, 5], ALU.add))
                        link(dve.tensor_tensor(m1[:, 3, :], m1[:, 1, :], m1[:, 1, :], ALU.mult))
                        link(dve.tensor_scalar(m1[:, 2, :], m1[:, 2, :], 1.0 / P, EPS, ALU.mult, ALU.add))
                        dve.scalar_tensor_tensor(out=m1[:, 4, :], in0=m1[:, 3, :], scalar=0.25, in1=m1[:, 2, :],
                                                 op0=ALU.mult, op1=ALU.add).then_inc(var_ready[n + 1], 1)
                    return stage

                def layer_norm_apply(n, source):
                    def stage(b, arg):
                        m1 = moment1
                        dve.wait_ge(rstd_ready[n + 1], b + 1)
                        link(dve.scalar_tensor_tensor(out=m1[:, 6, :], in0=m1[:, 0, :], scalar=-0.5, in1=m1[:, 5, :],
                                                      op0=ALU.mult, op1=ALU.mult))
                        for i in range(tiles):
                            last = dve.tensor_scalar(work_tok[:, i, :], source[:, i, :], m1[:, 5, i:i + 1],
                                                     m1[:, 6, i:i + 1], ALU.mult, ALU.add)
                        last.then_inc(normed_ready[n], 1)
                    return stage

                def rqk_tokens(b, arg):
                    for half in range(halves):
                        bank = read_bank()
                        at = slice(half * tiles_per_half, (half + 1) * tiles_per_half)
                        dve.tensor_copy(rqk[:, at, :], bank.rearrange("p (i c) -> p i c", c=P))\
                           .then_inc(rqk_ready, 1)
                    dve.wait_ge(rqk_ready, halves * (b + 1))

                def den(b, phase):
                    dve.tensor_copy(den_sb[:, :], read_bank()).then_inc(den_evicted, 1)

                def retrieve_a(b, phase):
                    group, half = divmod(phase, halves)
                    banks.take()
                    bank = read_bank()
                    den_rows = bank.rearrange("p (m r) -> p m r", r=QUAD)[:, :, 0]
                    dve.tensor_copy(den_tok[:, :], den_rows).then_inc(den_tok_ready, 1)
                    dve.wait_ge(den_tok_ready, phases * b + phase + 1)
                    link(dve.reciprocal(small[:, 0, :], den_tok[:, :]))
                    dve.wait_ge(u_tok_ready, phases * b + phase + 1)
                    keys = rqk[:, half * tiles_per_half:(half + 1) * tiles_per_half,
                               group * GROUP * HEAD_DIM:(group + 1) * GROUP * HEAD_DIM]
                    link(dve.tensor_tensor(prod[:, 0, :, :].rearrange("p (i h) d -> p i h d", h=GROUP),
                                           u_tok[:, :, :, HEAD_DIM:], keys.rearrange("p i (h d) -> p i h d", d=HEAD_DIM),
                                           ALU.mult))
                    link(dve.tensor_reduce(small[:, 1, :], prod[:, 0, :, :], AXIS.X, ALU.add))
                    link(dve.tensor_tensor(small[:, 1, :], small[:, 1, :], small[:, 0, :], ALU.mult))
                    dve.tensor_scalar(small[:, 2, :], small[:, 1, :], -scale1, EXP_ARG_MAX, ALU.mult, ALU.min)\
                       .then_inc(gate_arg_ready, 1)

                def retrieve_b(b, phase):
                    group, half = divmod(phase, halves)
                    dve.wait_ge(gate_exp_ready, phases * b + phase + 1)
                    link(dve.tensor_scalar(small[:, 4, :], small[:, 3, :], 1.0, None, ALU.add))
                    link(dve.reciprocal(small[:, 5, :], small[:, 4, :]))
                    link(dve.tensor_tensor(small[:, 5, :], small[:, 5, :], small[:, 0, :], ALU.mult))
                    flat = u_tok[:, :, :, :].rearrange("p i h r -> p (i h) r")
                    wide = [P, tiles_per_half * GROUP, HEAD_DIM]
                    dve.tensor_tensor(prod[:, 0, :, :], flat[:, :, 0:HEAD_DIM],
                                      small[:, 0, :].unsqueeze(2).broadcast_to(wide), ALU.mult)
                    link(dve.tensor_tensor(prod[:, 1, :, :], flat[:, :, HEAD_DIM:],
                                           small[:, 5, :].unsqueeze(2).broadcast_to(wide), ALU.mult))
                    if phase == 0:
                        wait(dve, channels_ready[1], halves * b)
                    to = mixed[:, half * tiles_per_half:(half + 1) * tiles_per_half,
                               group * GROUP * HEAD_DIM:(group + 1) * GROUP * HEAD_DIM]
                    dve.tensor_tensor(to.rearrange("p i (h d) -> p i h d", d=HEAD_DIM),
                                      prod[:, 0, :, :].rearrange("p (i h) d -> p i h d", h=GROUP),
                                      prod[:, 1, :, :].rearrange("p (i h) d -> p i h d", h=GROUP),
                                      ALU.add).then_inc(mixed_ready, 1)

                def add_bank(ready):
                    def stage(b, arg):
                        for half in range(halves):
                            bank = read_bank()
                            at = slice(half * tiles_per_half, (half + 1) * tiles_per_half)
                            dve.tensor_tensor(t_core[:, at, :], t_core[:, at, :],
                                              bank.rearrange("p (i c) -> p i c", c=P), ALU.add).then_inc(ready, 1)
                        dve.wait_ge(ready, halves * (b + 1))
                    return stage

                def hold_tokens(b, arg):
                    link(dve.tensor_copy(t_held[:, :, :], t_front[:, :, :]))

                def take_tokens(b, arg):
                    wait(dve, out_ready, halves * b)
                    link(dve.tensor_copy(t_core[:, :, :], t_held[:, :, :]))

                stages = {
                    "norm_group_mean": norm_group_mean, "norm_group_var": norm_group_var, "norm_apply": norm_apply,
                    "q0": lower_part(q_hi[0], q_lo[0], 0), "k0": lower_part(k_hi[0], k_lo[0], 0),
                    "q1": lower_part(q_hi[1], q_lo[1], 1), "k1": lower_part(k_hi[1], k_lo[1], 1),
                    "max0": max0, "max1": max1,
                    "x_tokens": x_tokens, "value0": value0,
                    "ln1_stats": layer_norm_stats(0, t_front), "ln1_apply": layer_norm_apply(0, t_front),
                    "ln2_stats": layer_norm_stats(1, t_core), "ln2_apply": layer_norm_apply(1, t_core),
                    "rqk": rqk_tokens, "den": den,
                    "retrieve_a": retrieve_a, "retrieve_b": retrieve_b, "out1": add_bank(out1_added),
                    "ffn": add_bank(result_ready), "hold_tokens": hold_tokens,
                    "take_tokens": take_tokens,
                }
                in_order(dve, steps, images, stages, banks, links)

            with nc.Block() as block:
                @block.sync
                def _(sp):
                    sync_program(sp)

                @block.gpsimd
                def _(pool):
                    gpsimd_program(pool)

                @block.tensor
                def _(pe):
                    tensor_program(pe)

                @block.scalar
                def _(act):
                    scalar_program(act)

                @block.vector
                def _(dve):
                    vector_program(dve)

        all_images()


_INS = ["x", "L0_conv_norm_w", "L0_conv_norm_b", "L0_conv_qkv_w", "L0_conv_qkv_b", "L0_conv_proj_w",
        "L0_conv_proj_b", "L1_attn_wq_s", "L1_attn_wk_s", "L1_attn_wv_r", "L1_attn_wq_r", "L1_attn_wk_ret",
        "L1_attn_w_out", "L1_ffn_qidx", "L1_ffn_scales", "L1_ffn_W"]


def kernel(**inputs):
    import concourse.bacc as bacc
    from concourse.bass_utils import run_bass_kernel_spmd

    nc = bacc.Bacc("TRN2", target_bir_lowering=False, num_devices=1)
    arrays, args = {}, []
    for name in _INS:
        a = np.ascontiguousarray(inputs[name])
        arrays[f"in_{name}"] = a
        args.append(nc.dram_tensor(f"in_{name}", a.shape, mybir.dt.from_np(a.dtype), kind="ExternalInput").ap())
    shape = inputs["x"].shape
    args.append(nc.dram_tensor("out_y", shape, F32, kind="ExternalOutput").ap())
    build(nc, *args)
    result = run_bass_kernel_spmd(nc, [arrays], core_ids=[0])
    return result.results[0]["out_y"]
```

```python
from contextlib import ExitStack

import numpy as np

import concourse.bass as bass
from concourse import mybir

F32 = mybir.dt.float32
F32R = mybir.dt.float32r
I32 = mybir.dt.int32
ALU = mybir.AluOpType
ACT = mybir.ActivationFunctionType
AXIS = mybir.AxisListType

P = 128
HALF = 512
HEADS = 8
HEAD_DIM = 16
RETRIEVERS = 2
PAIRS = HEADS // 2
GROUP = 4
QUAD = 32
GROUPS_L0 = 8
EPS = 1e-5
EXP_ARG_MAX = 80.0
NF4 = [-1.0, -0.6961928009986877, -0.5250730514526367, -0.39491748809814453, -0.28444138169288635,
       -0.18477343022823334, -0.09105003625154495, 0.0, 0.07958029955625534, 0.16093020141124725,
       0.24611230194568634, 0.33791524171829224, 0.44070982933044434, 0.5626170039176941,
       0.7229568362236023, 1.0]
NF4_BLOCK = 16

VECTOR_LINKS = 61
BANKS = 7
VECTOR_LOAD = {"turn_sums": 0.3, "gate_arg": 3, "retrieve": 3, "out1": 3.5, "ffn": 2, "ln2_stats": 1.5,
               "ln1_stats": 1.5, "ln1_apply": 0.3, "ln2_apply": 0.3, "q0": 2.2, "k0": 2.2, "q1": 2, "k1": 2,
               "x_tokens": 2, "value0": 1.2, "max0": 2, "hold_tokens": 1, "take_tokens": 1, "norm_stats": 2,
               "norm_means": 1, "norm_moments": 1, "norm_group_mean": 1, "norm_apply": 1.7}
LAST_STEP_LOAD = 5
TENSOR_LOAD = {"den": 1.8, "turn_sums": 0.9, "rqk": 1.7, "mixed_channels": 0.9, "out1": 1.7, "ln2_channels": 0.9,
               "ffn": 1.7, "result": 0.9, "score0": 0.9, "value0": 1.75, "ln1_channels": 0.9, "q1": 1.7, "k1": 1.7,
               "rv": 1.7, "q0": 1.7, "k0": 1.7, "v0": 1.7, "max0": 0.45, "x_tokens": 0.9, "max_rows0": 0.9,
               "max_rows1": 0.45, "values": 0.95}
VALUES_AT = 0.3
SCORES_AT = 0.08
SCORES_SPREAD = 0.18
AHEAD = {"TAIL": -1, "HEAD": 0, "FRONT": 1, "NEXT": 2}


def banks_of(stage):
    return {
        "norm_group_mean": 1, "norm_group_var": 1, "q0": 2, "k0": 2, "v0": 2, "max0": 2, "max_rows0": 2,
        "score0": 1, "x_tokens": 2, "value0": 1, "ln1_channels": 2, "q1": 2, "k1": 2, "rv": 1,
        "scores": 1, "max1": 1, "max_rows1": 1, "rqk": 2, "den": 1, "turn_sums": 2, "mixed_channels": 2, "out1": 2,
        "ln2_channels": 2, "ffn": 2, "result": 2,
    }.get(stage, 0)


def schedule():
    steps = [[] for _ in range(32)]

    def put(step, image, stage, arg=0):
        steps[step].append((image, stage, arg))

    for phase in range(4):
        start = 8 * ((phase + 1) % 4)
        image = "HEAD" if phase < 3 else "TAIL"
        put(start + 1, image, "evict_u", phase)
        put(start + 1, image, "den", phase)
        turn = start + (2 if phase == 3 else 3)
        put(turn, image, "turn_sums", phase)
        put(turn, image, "gate_arg", phase)
        put(turn + 1, image, "gate", phase)
        put(turn + 1, image, "retrieve", phase)
    put(1, "HEAD", "take_values")
    put(3, "HEAD", "rqk")
    put(4, "TAIL", "mixed_channels")
    put(5, "TAIL", "out1")
    put(5, "TAIL", "ln2_stats")
    for n in range(4):
        put(7 + n // 2, "TAIL", "ln2_apply", n)
        put(18, "FRONT", "ln1_apply", n)
    put(9, "TAIL", "ln2_channels")
    put(10, "TAIL", "ffn")
    put(12, "TAIL", "result")
    put(13, "HEAD", "take_tokens")
    for n, step in enumerate((29, 30, 30, 31, 31, 0, 0, 1, 8, 9, 10, 11, 11, 12, 12, 13)):
        put(step, "NEXT" if step > 16 else "FRONT", "score0", n)
    for n, step in enumerate((2, 4, 6, 7, 13, 14, 15, 16)):
        put(step, "FRONT", "value0", n)
    put(16, "FRONT", "ln1_stats")
    put(19, "FRONT", "ln1_channels")
    put(20, "FRONT", "q1")
    put(21, "FRONT", "k1")
    put(22, "FRONT", "hold_tokens")
    put(23, "FRONT", "rv")
    put(15, "NEXT", "norm_stats")
    put(16, "NEXT", "norm_means")
    put(16, "NEXT", "norm_moments")
    put(18, "NEXT", "norm_group_mean")
    put(19, "NEXT", "norm_group_var")
    put(20, "NEXT", "norm_apply")
    put(21, "NEXT", "q0")
    put(22, "NEXT", "k0")
    put(24, "NEXT", "v0")
    for n, step in enumerate((23, 23, 23, 24, 24, 25, 26, 26)):
        put(step, "NEXT", "max0", n)
    put(26, "NEXT", "x_tokens")
    put(28, "NEXT", "max_rows0")
    in_turn = []
    for phase in range(4):
        eight = range(8 * phase, 8 * phase + 8)
        ahead = (phase + 1) % 4
        image = "HEAD" if ahead else "FRONT"
        load = [sum(VECTOR_LOAD.get(stage, 0) for _, stage, _ in steps[step]) for step in eight]
        load[7] += LAST_STEP_LOAD
        count = [0] * 8
        for _ in range(32):
            least = min(range(8), key=lambda n: load[n] + count[n])
            count[least] += 1
        first = 0
        for n, step in enumerate(eight):
            maxima = [(image, "max1", (ahead, use)) for use in range(first, first + count[n])]
            first += count[n]
            early = [other for other in steps[step] if other[1] in ("gate", "evict_u", "take_values")]
            placed = [(0.0, one) for one in early]
            total = sum(TENSOR_LOAD.get(stage, 0) for _, stage, _ in steps[step]) or 1
            at = 0.0
            for one in steps[step]:
                if one[1] == "max_rows0":
                    placed.append((0.95, one))
                elif one[1] == "ln1_apply":
                    placed.append((0.1 + 0.22 * one[2], one))
                elif one[1] == "ln2_apply":
                    placed.append(((0.5, 0.65, 0.15, 0.35)[one[2]], one))
                elif one not in early:
                    placed.append((at / total, one))
                    at += TENSOR_LOAD.get(one[1], 0)
            behind = ("HEAD", "values", step - 1) if step else ("TAIL", "values", 31)
            placed.append((VALUES_AT if n else 0.02, behind))
            placed += [(SCORES_AT + SCORES_SPREAD * m, ("HEAD", "scores", (step, m))) for m in range(4)]
            end = 0.75 if n == 7 else 1.0
            placed += [(end * (m + 0.5) / len(maxima), one) for m, one in enumerate(maxima)]
            if n == 7:
                placed.append((0.85, (image, "max_rows1", ahead)))
            in_turn.append([one for _, one in sorted(placed, key=lambda item: item[0])])
    return in_turn


class Banks:

    def __init__(self):
        self.taken = 0
        self.looped = 0

    def take(self):
        bank, before = self.taken % BANKS, self.taken // BANKS + self.looped
        self.taken += 1
        return bank, before

    def skip(self, stage):
        self.taken += banks_of(stage)


class Links:

    def __init__(self, sem):
        self.sem = sem
        self.count = 0
        self.looped = 0

    def next(self):
        self.count += 1
        return self.count + self.looped


def wait(engine, sem, value):
    if not isinstance(value, int) or value > 0:
        engine.wait_ge(sem, value)


def in_order(engine, steps, images, stages, banks=None, links=None, first=None):

    def image_of(b, kinds):
        if first:
            first(b)
        for step in steps:
            for kind, stage, arg in step:
                if kind in kinds:
                    if stage in stages:
                        stages[stage](b + AHEAD[kind], arg)
                    elif banks:
                        banks.skip(stage)

    image_of(-2, ("NEXT",))
    image_of(-1, ("FRONT", "NEXT"))
    image_of(0, ("HEAD", "FRONT", "NEXT"))
    banks_per_image = sum(banks_of(stage) for step in steps for _, stage, _ in step)
    assert banks_per_image % BANKS == 0
    before = links.count if links else 0
    with engine.Fori(1, images - 2) as b:
        if banks:
            banks.looped = (b - 1) * (banks_per_image // BANKS)
        if links:
            links.looped = (b - 1) * VECTOR_LINKS
        image_of(b, tuple(AHEAD))
    if links:
        assert links.count - before == VECTOR_LINKS, links.count - before
        links.looped = (images - 4) * VECTOR_LINKS
    if banks:
        banks.looped = (images - 4) * (banks_per_image // BANKS)
    image_of(images - 2, ("HEAD", "TAIL", "FRONT"))
    image_of(images - 1, ("HEAD", "TAIL"))
    image_of(images, ("TAIL",))


def build(nc, x, norm_w, norm_b, qkv_w, qkv_b, proj_w, proj_b, wq_s, wk_s, wv_r, wq_r, wk_ret, w_out,
          qidx, scales, ffn_w, y):
    images, _, height, width = x.shape
    tokens = height * width
    tiles = tokens // P
    halves = tokens // HALF
    tiles_per_half = HALF // P
    scale0 = float(P) ** -0.5
    scale1 = float(HEAD_DIM) ** -0.5
    ring = 4
    phases = (HEADS // GROUP) * halves
    steps_per_image = phases * tiles
    adds = tiles - 2
    uses_per_phase = GROUP * tiles_per_half * halves
    stack_incs = 16 * 3 * 3 * (PAIRS // 2)
    x_dram = x.rearrange("b c h w -> b c (h w)")
    y_dram = y.rearrange("b c h w -> b c (h w)")

    with ExitStack() as ctx:
        def sb(name, shape, dtype=F32):
            return ctx.enter_context(nc.sbuf_tensor(name, shape, dtype))

        def psum(name, shape):
            return ctx.enter_context(nc.psum_tensor(name, shape, F32))

        def sem(name):
            return ctx.enter_context(nc.semaphore(name))

        ps_u = psum("ps_u", [P, HALF])
        ps_bank = psum("ps_bank", [P, BANKS, HALF])

        ident = sb("ident", [P, P])
        group_mean = sb("group_mean", [P, P])
        ones = sb("ones", [P, P])
        first_row = sb("first_row", [P, P], F32R)

        p0 = sb("p0", [P, tiles, HALF])
        setup_tiles = p0[:, :, :].rearrange("p a (b n) -> p (a b) n", n=P)
        qkv_rows = setup_tiles[:, 0:3, :]
        proj_rows, ffn_rows, wq_r_sb, wk_ret_blocks = (setup_tiles[:, n, :] for n in range(3, 7))
        bias_v, proj_bias, q_value, lora, lora_part = (setup_tiles[:, n, :] for n in range(7, 12))
        q_index = setup_tiles[:, 12, :].bitcast(I32)
        turned = setup_tiles[:, 13:17, :]
        qk_w = sb("qk_w", [P, 2, P])
        value_w = sb("value_w", [P, P])
        token_bias = sb("token_bias", [P, P])
        gate_w = sb("gate_w", [P, P])
        ffn_w_sb = sb("ffn_w_sb", [P, P])
        wq_sb = sb("wq_sb", [P, P])
        wk_sb = sb("wk_sb", [P, P])
        wv_r_sb = sb("wv_r_sb", [P, RETRIEVERS * HEAD_DIM])
        wv_sb = sb("wv_sb", [P, 4, QUAD])
        w_out_sb = sb("w_out_sb", [P, P])
        norm_cols = sb("norm_cols", [P, 2])
        qkv_bias = sb("qkv_bias", [P, 3])
        block_scale = sb("block_scale", [P, P // NF4_BLOCK])
        minus_half = sb("minus_half", [P, 8])

        x_sb = sb("x_sb", [P, tokens])
        stat0 = sb("stat0", [P, 2, 6])
        moment0 = sb("moment0", [P, 12])
        work = sb("work", [P, tokens])
        q_hi, q_lo, k_hi, k_lo = ([sb(f"{name}{layer}", [P, tokens], F32R) for layer in range(2)]
                                  for name in ("q_hi", "q_lo", "k_hi", "k_lo"))
        v0 = sb("v0", [P, tiles, P + 1])
        den0 = sb("den0", [P, tiles])
        t_front = sb("t_front", [P, tiles, P])
        t_held = sb("t_held", [P, tiles, P])
        t_core = sb("t_core", [P, tiles, P])

        stat1 = sb("stat1", [P, 2, tiles, 6])
        moment1 = sb("moment1", [P, 8, tiles])
        channels = sb("channels", [P, tokens])
        q_stack = sb("q_stack", [P, PAIRS, tokens], F32R)
        k_stack = sb("k_stack", [P, HEADS, tokens], F32R)
        rv_next = sb("rv_next", [P, tiles, QUAD])
        rv = sb("rv", [P, tiles, QUAD])
        rqk = sb("rqk", [P, tiles, P])
        p1 = sb("p1", [P, ring, GROUP, HALF])
        p_sum = sb("p_sum", [P, GROUP, HALF])
        u_sb = sb("u_sb", [P, HALF])
        den_sb = sb("den_sb", [P, HALF])
        u_tok = sb("u_tok", [P, tiles_per_half, GROUP, QUAD])
        den_tok = sb("den_tok", [P, tiles_per_half * GROUP])
        small = sb("small", [P, 6, tiles_per_half * GROUP])
        prod = sb("prod", [P, 2, tiles_per_half * GROUP, HEAD_DIM])
        work_tok = work[:, :].rearrange("p (i c) -> p i c", c=P)
        start_mark = sb("start_mark", [P, 2])
        part_dev = sb("part_dev", [P, 2 * halves])
        max_part0 = sb("max_part0", [P, tiles, halves])
        max_cols0 = sb("max_cols0", [P, tiles, QUAD])
        max_row0 = sb("max_row0", [P, tokens], F32R)
        max_part1 = sb("max_part1", [P, tiles_per_half, GROUP, halves])
        max_cols1 = sb("max_cols1", [P, tiles_per_half, QUAD])
        mixed = sb("mixed", [P, tiles, P])
        out_sb = sb("out_sb", [P, tokens])

        weights_loaded = sem("weights_loaded")
        blocks_zeroed = sem("blocks_zeroed")
        pool_ready = sem("pool_ready")
        pool_link = sem("pool_link")
        turned_filled = sem("turned_filled")
        turned_ready = sem("turned_ready")
        folded_filled = sem("folded_filled")
        dve_setup = sem("dve_setup")
        weights_ready = sem("weights_ready")

        with nc.Block() as block:
            @block.sync
            def _(sp):
                loads = [
                    (qkv_rows, qkv_w.rearrange("(t o) c -> o t c", o=P)),
                    (proj_rows, proj_w), (ffn_rows, ffn_w), (wq_r_sb, wq_r),
                    (wq_sb[:, :], wq_s), (wk_sb[:, :], wk_s), (wv_r_sb[:, :], wv_r),
                    (w_out_sb[:, :], w_out), (q_index, qidx),
                    (block_scale[:, :], scales.rearrange("(o k) -> o k", o=P)),
                    (norm_cols[:, 0:1], norm_w.rearrange("(c a) -> c a", a=1)),
                    (norm_cols[:, 1:2], norm_b.rearrange("(c a) -> c a", a=1)),
                    (proj_bias, proj_b.partition_broadcast(P)),
                ]
                for to, source in loads:
                    sp.dma_start(to, source).then_inc(weights_loaded, 16)
                with nc.allow_non_contiguous_dma(reason="384 biases, once"):
                    sp.dma_start(qkv_bias[:, :], qkv_b.rearrange("(t o) -> o t", o=P)).then_inc(weights_loaded, 16)
                sp.wait_ge(blocks_zeroed, 1)
                for h in range(HEADS):
                    rows = slice(h * HEAD_DIM, (h + 1) * HEAD_DIM)
                    sp.dma_start(wk_ret_blocks[rows, rows], wk_ret).then_inc(weights_loaded, 16)

            @block.gpsimd
            def _(pool):
                links = Links(pool_link)

                def link(instruction):
                    instruction.then_inc(links.sem, 1)
                    pool.wait_ge(links.sem, links.next())

                pool.memset(wk_ret_blocks, 0.0).then_inc(blocks_zeroed, 1)
                pool.memset(minus_half[:, :], -0.5)
                pool.memset(ones[:, :], 1.0)
                link(pool.memset(ident[:, :], 0.0))
                link(pool.affine_select(out=ident[:, :], in_=ident[:, :], compare_op=ALU.not_equal, fill=1.0,
                                        base=0, pattern=[[-1, P]], channel_multiplier=1))
                size = P // GROUPS_L0
                blocks = group_mean[:, :].rearrange("p (g c) -> p g c", g=GROUPS_L0)
                link(pool.memset(group_mean[:, :], 1.0 / size))
                link(pool.affine_select(out=blocks, in_=blocks, compare_op=ALU.is_ge, fill=0.0, base=0,
                                        pattern=[[-size, GROUPS_L0], [0, size]], channel_multiplier=1))
                link(pool.affine_select(out=blocks, in_=blocks, compare_op=ALU.is_ge, fill=0.0, base=size - 1,
                                        pattern=[[size, GROUPS_L0], [0, size]], channel_multiplier=-1))
                pool.memset(v0[:, :, P:P + 1], 1.0).then_inc(pool_ready, 1)
                pool.wait_ge(weights_loaded, 16 * (14 + HEADS))
                link(pool.tensor_copy(q_value, q_index))
                link(pool.memset(lora, 0.0))
                for n, value in enumerate(NF4):
                    link(pool.tensor_scalar(lora_part, q_value, float(n), float(value),
                                            ALU.is_equal, ALU.mult))
                    link(pool.tensor_tensor(lora, lora, lora_part, ALU.add))
                pool.tensor_tensor(lora.rearrange("p (k j) -> p k j", j=NF4_BLOCK),
                                   lora.rearrange("p (k j) -> p k j", j=NF4_BLOCK),
                                   block_scale[:, :].unsqueeze(2).broadcast_to([P, P // NF4_BLOCK, NF4_BLOCK]),
                                   ALU.mult).then_inc(pool_ready, 1)

            @block.tensor
            def _(pe):
                scratch = ps_bank[:, 1:3, :].rearrange("p a n -> p (a n)")
                pe.wait_ge(pool_ready, 1)
                pe.wait_ge(weights_loaded, 16 * (14 + HEADS))
                for n, source in enumerate((qkv_rows[:, 0, :], qkv_rows[:, 1, :], proj_rows,
                                            ffn_rows, wq_r_sb, wk_ret_blocks)):
                    last = pe.transpose(scratch[:, n * P:(n + 1) * P], source, ident[:, :])
                last.then_inc(turned_filled, 1)
                pe.wait_ge(turned_ready, 1)
                pe.wait_ge(pool_ready, 2)
                for n, (left, right) in enumerate((
                        (qkv_rows[:, 2, :], turned[:, 0, :]),
                        (bias_v, turned[:, 0, :]),
                        (turned[:, 2, :], turned[:, 3, :]),
                        (lora, turned[:, 1, :]))):
                    last = pe.matmul(ps_bank[:, 0, n * P:(n + 1) * P], left, right, start=True, stop=True)
                last.then_inc(folded_filled, 1)

            @block.vector
            def _(dve):
                links = Links(dve_setup)

                def link(instruction):
                    instruction.then_inc(links.sem, 1)
                    dve.wait_ge(links.sem, links.next())

                dve.memset(max_cols0[:, :, :], 0.0)
                dve.memset(max_cols1[:, :, :], 0.0)
                dve.memset(max_row0[:, :].bitcast(F32), 0.0)
                dve.memset(q_stack[:, :, :].bitcast(F32), 0.0)
                link(dve.memset(k_stack[:, :, :].bitcast(F32), 0.0))
                dve.wait_ge(pool_ready, 1)
                dve.tensor_copy(first_row[:, :], ident[:, 0:1].broadcast_to([P, P]))
                for head in range(HEADS):
                    row = 3 * QUAD + head % GROUP
                    dve.tensor_copy(k_stack[3 * QUAD:, head, :],
                                    ident[3 * QUAD:, row:row + 1].broadcast_to([QUAD, tokens]))
                dve.wait_ge(weights_loaded, 16 * (14 + HEADS))
                dve.tensor_scalar(bias_v, ones[:, :], qkv_bias[:, 2:3], None, ALU.mult)
                for n in range(4):
                    dve.tensor_copy(wv_sb[:, n, 0:HEAD_DIM], wv_r_sb[:, HEAD_DIM:])
                    dve.tensor_tensor(wv_sb[:, n, HEAD_DIM:], wv_r_sb[:, 0:HEAD_DIM], wv_r_sb[:, HEAD_DIM:],
                                      ALU.subtract)
                dve.wait_ge(turned_filled, 1)
                scratch = ps_bank[:, 1:3, :].rearrange("p a n -> p (a n)")
                dve.tensor_copy(qk_w[:, :, :].rearrange("p a n -> p (a n)"), scratch[:, 0:2 * P])
                dve.tensor_copy(turned.rearrange("p a n -> p (a n)"), scratch[:, 2 * P:6 * P])\
                   .then_inc(turned_ready, 1)
                dve.wait_ge(folded_filled, 1)
                dve.tensor_copy(value_w[:, :], ps_bank[:, 0, 0:P])
                dve.tensor_tensor(token_bias[:, :], ps_bank[:, 0, P:2 * P], proj_bias, ALU.add)
                dve.tensor_copy(gate_w[:, :], ps_bank[:, 0, 2 * P:3 * P])
                dve.tensor_copy(ffn_w_sb[:, :], ps_bank[:, 0, 3 * P:4 * P]).then_inc(weights_ready, 1)

        def all_images():
            steps = schedule()

            x_loaded = sem("x_loaded")
            stored = sem("stored")
            bank_filled = [sem(f"bank{n}_filled") for n in range(BANKS)]
            mean_read = sem("mean_read")
            value0_added = sem("value0_added")
            rqk_ready = sem("rqk_ready")
            den_tok_ready = sem("den_tok_ready")
            out1_added = sem("out1_added")
            dve_link = sem("dve_link")
            moments_ready = sem("moments_ready")
            spread_ready = sem("spread_ready")
            var_ready = [sem(f"var{n}_ready") for n in range(3)]
            rstd_ready = [sem(f"rstd{n}_ready") for n in range(3)]
            h_ready = sem("h_ready")
            hi_ready = [sem(f"hi{n}_ready") for n in range(2)]
            lo_ready = [sem(f"lo{n}_ready") for n in range(2)]
            v0_ready = sem("v0_ready")
            p0_ready = sem("p0_ready")
            x_used = sem("x_used")
            shift_ready = [sem(f"shift{n}_ready") for n in range(2)]
            normed_ready = [sem(f"normed{n}_ready") for n in range(2)]
            channels_ready = [sem(f"channels{n}_ready") for n in range(3)]
            rv_next_ready = sem("rv_next_ready")
            rv_ready = sem("rv_ready")
            p1_ready = sem("p1_ready")
            p1_summed = sem("p1_summed")
            values_done = sem("values_done")
            u_evicted = sem("u_evicted")
            p_sum_used = sem("p_sum_used")
            den_evicted = sem("den_evicted")
            u_tok_ready = sem("u_tok_ready")
            gate_arg_ready = sem("gate_arg_ready")
            gate_exp_ready = sem("gate_exp_ready")
            mixed_ready = sem("mixed_ready")
            result_ready = sem("result_ready")
            out_ready = sem("out_ready")
            maxed = [sem(f"maxed{n}") for n in range(2)]
            max_ready = [sem(f"max{n}_ready") for n in range(2)]
            max_row_ready = [sem(f"max_row{n}_ready") for n in range(2)]
            stacked = [sem(f"stacked{n}") for n in range(2)]

            def sync_program(sp):
                def load(b):
                    wait(sp, x_used, halves * b)
                    sp.dma_start(x_sb[:, :], x_dram[bass.ds(b, 1), :, :].rearrange("b c n -> (b c) n"))\
                      .then_inc(x_loaded, 16)

                def stack(b, group):
                    sp.wait_ge(lo_ready[1], 2 * halves * (b + 1))
                    wait(sp, p1_ready, GROUP * (steps_per_image * (b - 1) + (group + 1) * steps_per_image // 2))
                    for pair in range(group * PAIRS // 2, (group + 1) * PAIRS // 2):
                        for part, (q_part, k_part) in enumerate(((q_hi, k_hi), (q_hi, k_lo), (q_lo, k_hi))):
                            sp.dma_start(q_stack[part * QUAD:(part + 1) * QUAD, pair, :].bitcast(F32),
                                         q_part[1][pair * QUAD:(pair + 1) * QUAD, :].bitcast(F32))\
                              .then_inc(stacked[group], 16)
                            for n in range(2):
                                at, row = pair * QUAD + n * HEAD_DIM, part * QUAD + n * HEAD_DIM
                                sp.dma_start(k_stack[row:row + HEAD_DIM, 2 * pair + n, :].bitcast(F32),
                                             k_part[1][at:at + HEAD_DIM, :].bitcast(F32))\
                                  .then_inc(stacked[group], 16)

                def store(b):
                    sp.wait_ge(out_ready, halves * (b + 1))
                    sp.dma_start(y_dram[bass.ds(b, 1), :, :].rearrange("b c n -> (b c) n"), out_sb[:, :])\
                      .then_inc(stored, 16)

                load(0)
                load(1)
                stack(0, 0)
                stack(0, 1)
                load(2)
                stack(1, 0)
                load(3)
                with sp.Fori(1, images - 3) as b:
                    stack(b, 1)
                    store(b - 1)
                    stack(b + 1, 0)
                    load(b + 3)
                stack(images - 3, 1)
                store(images - 4)
                stack(images - 2, 0)
                stack(images - 2, 1)
                store(images - 3)
                stack(images - 1, 0)
                stack(images - 1, 1)
                store(images - 2)
                store(images - 1)
                sp.wait_ge(stored, 16 * (images + 1))

            def gpsimd_program(pool):
                def rstd(n):
                    def stage(b, arg):
                        width = 1 if n == 0 else tiles
                        into = moment0[:, 8:9] if n == 0 else moment1[:, 5, :]
                        of = moment0[:, 7:8] if n == 0 else moment1[:, 4, :]
                        pool.wait_ge(var_ready[n], b + 1)
                        pool.tensor_tensor(into, of, minus_half[:, 0:width], ALU.pow).then_inc(rstd_ready[n], 1)
                    return stage

                pool.memset(start_mark[:, :], 0.0).then_inc(stored, 16)

                def add_weights(b, step):
                    phase, key_tile = divmod(step, tiles)
                    if not 1 <= key_tile <= adds:
                        return
                    pool.wait_ge(p1_ready, GROUP * (steps_per_image * b + step + 1))
                    if key_tile == 1:
                        wait(pool, p_sum_used, phases * b + phase)
                    else:
                        pool.wait_ge(p1_summed, adds * (phases * b + phase) + key_tile - 1)
                    before = p1[:, (step - 1) % ring, :, :] if key_tile == 1 else p_sum[:, :, :]
                    pool.tensor_tensor(p_sum[:, :, :], before, p1[:, step % ring, :, :], ALU.add)\
                        .then_inc(p1_summed, 1)

                in_order(pool, steps, images, {"values": add_weights, "norm_group_var": rstd(0),
                                               "ln1_stats": rstd(1), "ln2_stats": rstd(2)})

            def tensor_program(pe):
                banks = Banks()

                readers = []
                uses_before = []

                def open_bank(reader, value, *awaited):
                    bank, _ = banks.take()
                    if len(readers) >= BANKS and not any(readers[-BANKS][0] is sem for sem in awaited):
                        pe.wait_ge(*readers[-BANKS])
                    readers.append((reader, value))
                    return ps_bank[:, bank, :], bank_filled[bank]

                def first_of_image(b):
                    looped = not isinstance(b, int)
                    if looped or b == 0:
                        uses_before.append(len(readers))
                    if looped or b == images - 2:
                        image_0 = readers[slice(*uses_before)]
                        for reader, value in image_0[-BANKS:]:
                            each = sum(other is reader for other, _ in image_0)
                            readers.append((reader, value + (b - 1) * each))

                def group_mean_of(b, arg):
                    pe.wait_ge(moments_ready, b + 1)
                    out, filled = open_bank(mean_read, b + 1)
                    pe.matmul(out[:, 0:2], group_mean[:, :], moment0[:, 0:2], start=True, stop=True)\
                      .then_inc(filled, 1)

                def group_var_of(b, arg):
                    pe.wait_ge(spread_ready, b + 1)
                    out, filled = open_bank(var_ready[0], b + 1)
                    pe.matmul(out[:, 0:1], group_mean[:, :], moment0[:, 5:6], start=True, stop=True)\
                      .then_inc(filled, 1)

                def project(weight, source, ready, count, reader, per_image, order):
                    def stage(b, arg):
                        pe.wait_ge(ready, count * (b + 1))
                        for half in range(halves):
                            out, filled = open_bank(reader, per_image * b + order + half + 1, ready)
                            pe.matmul(out, weight, source[:, half * HALF:(half + 1) * HALF],
                                      start=True, stop=True).then_inc(filled, 1)
                    return stage

                def project_tokens(weight, source, ready, count, reader):
                    def stage(b, arg):
                        pe.wait_ge(ready, count * (b + 1))
                        for half in range(halves):
                            out, filled = open_bank(reader, halves * b + half + 1, ready)
                            for i in range(tiles_per_half):
                                at = half * HALF + i * P
                                last = pe.matmul(out[:, i * P:(i + 1) * P], source[:, at:at + P], weight,
                                                 start=True, stop=True)
                            last.then_inc(filled, 1)
                    return stage

                def project_values(b, arg):
                    pe.wait_ge(channels_ready[0], halves * (b + 1))
                    out, filled = open_bank(rv_next_ready, b + 1, channels_ready[0])
                    for i in range(tiles):
                        last = pe.matmul(out[:, i * QUAD:i * QUAD + P], channels[:, i * P:(i + 1) * P],
                                         wv_sb[:, :, :].rearrange("c a n -> c (a n)"), start=True, stop=True)
                    last.then_inc(filled, 1)

                def turn(source, ready, count, reader):
                    def stage(b, arg):
                        pe.wait_ge(ready, count * (b + 1))
                        for half in range(halves):
                            out, filled = open_bank(reader, halves * b + half + 1, ready)
                            for i in range(tiles_per_half):
                                last = pe.transpose(out[:, i * P:(i + 1) * P],
                                                    source[:, half * tiles_per_half + i, :], ident[:, :])
                            last.then_inc(filled, 1)
                    return stage

                def max0(b, i):
                    if i == 0:
                        pe.wait_ge(lo_ready[0], 2 * halves * (b + 1))
                    for half in range(halves):
                        out, filled = open_bank(maxed[0], halves * (tiles * b + i) + half + 1,
                                                *((lo_ready[0],) if i == 0 else ()))
                        pe.matmul(out, q_hi[0][:, i * P:(i + 1) * P], k_hi[0][:, half * HALF:(half + 1) * HALF],
                                  start=True, stop=True).then_inc(filled, 1)

                def max_rows0(b, arg):
                    pe.wait_ge(max_ready[0], b + 1)
                    for half in range(halves):
                        out, filled = open_bank(max_row_ready[0], halves * b + half + 1)
                        for i in range(tiles_per_half):
                            last = pe.transpose(out[0:QUAD, i * P:(i + 1) * P],
                                                max_cols0[:, half * tiles_per_half + i, :], ident[:, :])
                        last.then_inc(filled, 1)

                def score0(b, n):
                    half, key_tile = divmod(n, tiles)
                    if n == 0:
                        pe.wait_ge(max_row_ready[0], halves * (b + 1))
                    out, filled = open_bank(p0_ready, halves * tiles * b + n + 1, *((max_row_ready[0],) if n == 0 else ()))
                    keys, queries = slice(key_tile * P, (key_tile + 1) * P), slice(half * HALF, (half + 1) * HALF)
                    pe.matmul(out, k_hi[0][:, keys], q_hi[0][:, queries], start=True, stop=False)
                    pe.matmul(out, k_hi[0][:, keys], q_lo[0][:, queries], start=False, stop=False)
                    pe.matmul(out, first_row[:, :], max_row0[:, queries], start=False, stop=False)
                    pe.matmul(out, k_lo[0][:, keys], q_hi[0][:, queries], start=False, stop=True).then_inc(filled, 1)

                def value0(b, query_tile):
                    awaited = ()
                    if query_tile % tiles_per_half == 0:
                        half = query_tile // tiles_per_half
                        pe.wait_ge(v0_ready, halves * (b + 1))
                        pe.wait_ge(p0_ready, tiles * (halves * b + half + 1))
                        awaited = (v0_ready, p0_ready)
                    out, filled = open_bank(value0_added, tiles * b + query_tile + 1, *awaited)
                    at = query_tile % tiles_per_half * P
                    for key_tile in range(tiles):
                        last = pe.matmul(out[:, 0:P + 1], p0[:, key_tile, at:at + P], v0[:, key_tile, :],
                                         start=(key_tile == 0), stop=(key_tile == tiles - 1))
                    last.then_inc(filled, 1)

                def max1(b, arg):
                    phase, use = arg
                    group, q_half = divmod(phase, halves)
                    if use == 0:
                        pe.wait_ge(stacked[group], stack_incs * (b + 1))
                    i, n, half = use // (GROUP * halves), use // halves % GROUP, use % halves
                    head, at = group * GROUP + n, (q_half * tiles_per_half + i) * P
                    out, filled = open_bank(maxed[1], uses_per_phase * (phases * b + phase) + use + 1)
                    pe.matmul(out, q_stack[0:3 * QUAD, head // 2, at:at + P],
                              k_stack[0:3 * QUAD, head, half * HALF:(half + 1) * HALF],
                              start=True, stop=True).then_inc(filled, 1)

                def max_rows1(b, phase):
                    pe.wait_ge(max_ready[1], phases * b + phase + 1)
                    out, filled = open_bank(max_row_ready[1], phases * b + phase + 1)
                    for i in range(tiles_per_half):
                        last = pe.transpose(out[0:QUAD, i * P:(i + 1) * P], max_cols1[:, i, :], ident[:, :])
                    last.then_inc(filled, 1)

                def scores(b, arg):
                    step, n = arg
                    phase, key_tile = divmod(step, tiles)
                    group, half = divmod(phase, halves)
                    queries, keys = slice(half * HALF, (half + 1) * HALF), slice(key_tile * P, (key_tile + 1) * P)
                    awaited = ()
                    if key_tile == 0 and n == 0:
                        pe.wait_ge(max_row_ready[1], phases * b + phase + 1)
                        awaited = (max_row_ready[1],)
                    out, filled = open_bank(p1_ready, GROUP * (steps_per_image * b + step) + n + 1, *awaited)
                    head = GROUP * group + n
                    pe.matmul(out, k_stack[:, head, keys], q_stack[:, head // 2, queries], start=True, stop=True)\
                      .then_inc(filled, 1)

                def sum_values(b, step):
                    phase, key_tile = divmod(step, tiles)
                    if step == 0:
                        pe.wait_ge(rv_ready, b + 1)
                    if key_tile == 0:
                        wait(pe, u_evicted, phases * b + phase)
                    pe.wait_ge(p1_ready, GROUP * (steps_per_image * b + step + 1))
                    for n in range(GROUP):
                        last = pe.matmul(ps_u[n * QUAD:(n + 1) * QUAD, :], rv[:, key_tile, :],
                                         p1[:, step % ring, n, :], start=(key_tile == 0),
                                         stop=(key_tile == tiles - 1))
                    last.then_inc(values_done, 1)

                def den(b, phase):
                    pe.wait_ge(p1_summed, adds * (phases * b + phase + 1))
                    out, filled = open_bank(den_evicted, phases * b + phase + 1)
                    last_weights = p1[:, (phase * tiles + tiles - 1) % ring, :, :]
                    for source in (p_sum, last_weights):
                        for n in range(GROUP):
                            last = pe.matmul(out[n * QUAD:(n + 1) * QUAD, :], ones[:, 0:QUAD], source[:, n, :],
                                             start=(source is p_sum), stop=(source is last_weights))
                        last.then_inc(p_sum_used if source is p_sum else filled, 1)

                def turn_sums(b, phase):
                    for source, ready, reader in ((u_sb, u_evicted, u_tok_ready), (den_sb, den_evicted, den_tok_ready)):
                        pe.wait_ge(ready, phases * b + phase + 1)
                        out, filled = open_bank(reader, phases * b + phase + 1, ready)
                        for i in range(tiles_per_half):
                            last = pe.transpose(out[:, i * P:(i + 1) * P], source[:, i * P:(i + 1) * P], ident[:, :])
                        last.then_inc(filled, 1)

                stages = {
                    "norm_group_mean": group_mean_of, "norm_group_var": group_var_of,
                    "q0": project(qk_w[:, 0, :], work, h_ready, 1, lo_ready[0], 2 * halves, 0),
                    "k0": project(qk_w[:, 1, :], work, h_ready, 1, lo_ready[0], 2 * halves, halves),
                    "v0": project_tokens(value_w[:, :], work, h_ready, 1, v0_ready),
                    "max0": max0, "max_rows0": max_rows0, "score0": score0,
                    "x_tokens": turn(x_sb[:, :].rearrange("c (i n) -> c i n", n=P), x_loaded, 16, x_used),
                    "value0": value0,
                    "ln1_channels": turn(work_tok, normed_ready[0], 4, channels_ready[0]),
                    "q1": project(wq_sb[:, :], channels, channels_ready[0], halves, lo_ready[1], 2 * halves, 0),
                    "k1": project(wk_sb[:, :], channels, channels_ready[0], halves, lo_ready[1], 2 * halves, halves),
                    "rv": project_values,
                    "max1": max1, "max_rows1": max_rows1,
                    "rqk": project_tokens(gate_w[:, :], channels, channels_ready[0], halves, rqk_ready),
                    "scores": scores, "values": sum_values, "den": den, "turn_sums": turn_sums,
                    "mixed_channels": turn(mixed, mixed_ready, phases, channels_ready[1]),
                    "out1": project_tokens(w_out_sb[:, :], channels, channels_ready[1], halves, out1_added),
                    "ln2_channels": turn(work_tok, normed_ready[1], 4, channels_ready[2]),
                    "ffn": project_tokens(ffn_w_sb[:, :], channels, channels_ready[2], halves, result_ready),
                    "result": turn(t_core, result_ready, halves, out_ready),
                }
                in_order(pe, steps, images, stages, banks, first=first_of_image)

            def scalar_program(act):
                banks = Banks()

                def read_bank():
                    bank, before = banks.take()
                    act.wait_ge(bank_filled[bank], before + 1)
                    return ps_bank[:, bank, :]

                def halves_to(of_half, ready):
                    def stage(b, arg):
                        for half in range(halves):
                            bank = read_bank()
                            to, columns = of_half(half)
                            act.copy(to, columns(bank)).then_inc(ready, 1)
                    return stage

                def upper_part(to, layer):
                    def stage(b, arg):
                        if layer:
                            for group in range(2):
                                wait(act, stacked[group], stack_incs * b)
                        for half in range(halves):
                            bank = read_bank()
                            at = slice(half * HALF, (half + 1) * HALF)
                            bias = 0.0 if layer else qkv_bias[:, (0 if to is q_hi[0] else 1):(1 if to is q_hi[0] else 2)]
                            act.activation(to[:, at], bank, ACT.Identity, bias=bias)\
                               .then_inc(hi_ready[layer], 1)
                    return stage

                def v0_part(half):
                    return (v0[:, half * tiles_per_half:(half + 1) * tiles_per_half, 0:P],
                            lambda bank: bank.rearrange("p (i c) -> p i c", c=P))

                def channels_part(half):
                    return channels[:, half * HALF:(half + 1) * HALF], lambda bank: bank

                def rv_values(b, arg):
                    act.copy(rv_next[:, :, :], read_bank()[:, 0:tiles * QUAD].rearrange("p (i n) -> p i n", n=QUAD))\
                       .then_inc(rv_next_ready, 1)

                def score0(b, n):
                    if n % tiles == 0:
                        wait(act, value0_added, tiles_per_half * (halves * b + n // tiles))
                    act.activation(p0[:, n % tiles, :], read_bank(), ACT.Exp, scale=scale0).then_inc(p0_ready, 1)

                def max_rows0(b, arg):
                    for half in range(halves):
                        act.copy(max_row0[0:QUAD, half * HALF:(half + 1) * HALF], read_bank()[0:QUAD, :])\
                           .then_inc(max_row_ready[0], 1)

                def max_rows1(b, phase):
                    group, half = divmod(phase, halves)
                    pairs = slice(group * GROUP // 2, (group + 1) * GROUP // 2)
                    act.copy(q_stack[3 * QUAD:, pairs, half * HALF:(half + 1) * HALF],
                             read_bank()[0:QUAD, :].unsqueeze(1).broadcast_to([QUAD, GROUP // 2, HALF]))\
                       .then_inc(max_row_ready[1], 1)

                def rqk_part(half):
                    return (rqk[:, half * tiles_per_half:(half + 1) * tiles_per_half, :],
                            lambda bank: bank.rearrange("p (i c) -> p i c", c=P))

                def normalise(n, source):
                    def stage(b, part):
                        if part == 0:
                            act.wait_ge(shift_ready[n], b + 1)
                        for i in range(part * tiles // 4, (part + 1) * tiles // 4):
                            last = act.activation(work_tok[:, i, :], source[:, i, :], ACT.Identity,
                                                  scale=moment1[:, 5, i:i + 1], bias=moment1[:, 6, i:i + 1])
                        last.then_inc(normed_ready[n], 1)
                    return stage

                def take_values(b, arg):
                    act.wait_ge(rv_next_ready, b + 1)
                    wait(act, values_done, steps_per_image * b)
                    act.copy(rv[:, :, :], rv_next[:, :, :]).then_inc(rv_ready, 1)

                def weights(b, arg):
                    step, n = arg
                    done = steps_per_image * b + step
                    if n == 0:
                        wait(act, values_done, done - ring + 1)
                        phase, key_tile = divmod(step - ring, tiles)
                        if key_tile <= adds:
                            wait(act, p1_summed, adds * (phases * b + phase) + max(key_tile, 1))
                        else:
                            wait(act, den_evicted, phases * b + phase + 1)
                    act.activation(p1[:, step % ring, n, :], read_bank(), ACT.Exp, scale=scale1)\
                       .then_inc(p1_ready, 1)

                def evict_u(b, phase):
                    act.wait_ge(values_done, tiles * (phases * b + phase + 1))
                    act.copy(u_sb[:, :], ps_u[:, :]).then_inc(u_evicted, 1)

                def den(b, phase):
                    act.copy(den_sb[:, :], read_bank()).then_inc(den_evicted, 1)

                def turn_sums(b, phase):
                    bank = read_bank()
                    wait(act, mixed_ready, phases * b + phase)
                    act.copy(u_tok[:, :, :, :].rearrange("p i h r -> p (i h r)"), bank)\
                       .then_inc(u_tok_ready, 1)
                    banks.take()

                def gate(b, phase):
                    act.wait_ge(gate_arg_ready, phases * b + phase + 1)
                    act.activation(small[:, 3, :], small[:, 2, :], ACT.Exp).then_inc(gate_exp_ready, 1)

                def result(b, arg):
                    act.wait_ge(stored, 16 * (b + 1))
                    for half in range(halves):
                        bank = read_bank()
                        act.copy(out_sb[:, half * HALF:(half + 1) * HALF], bank)\
                           .then_inc(out_ready, 1)

                stages = {
                    "q0": upper_part(q_hi[0], 0), "k0": upper_part(k_hi[0], 0),
                    "v0": halves_to(v0_part, v0_ready), "score0": score0,
                    "ln1_channels": halves_to(channels_part, channels_ready[0]),
                    "q1": upper_part(q_hi[1], 1), "k1": upper_part(k_hi[1], 1),
                    "rv": rv_values,
                    "max_rows0": max_rows0, "max_rows1": max_rows1, "take_values": take_values,
                    "ln1_apply": normalise(0, t_front), "ln2_apply": normalise(1, t_core),
                    "rqk": halves_to(rqk_part, rqk_ready), "den": den,
                    "scores": weights, "evict_u": evict_u, "turn_sums": turn_sums, "gate": gate,
                    "mixed_channels": halves_to(channels_part, channels_ready[1]),
                    "ln2_channels": halves_to(channels_part, channels_ready[2]), "result": result,
                }
                in_order(act, steps, images, stages, banks)

            def vector_program(dve):
                banks, links = Banks(), Links(dve_link)

                def link(instruction):
                    instruction.then_inc(links.sem, 1)
                    dve.wait_ge(links.sem, links.next())

                def mark(instruction):
                    instruction.then_inc(links.sem, 1)
                    marked.append(links.next())

                def settle():
                    dve.wait_ge(links.sem, marked[-1])

                marked = []

                def read_bank():
                    bank, before = banks.take()
                    dve.wait_ge(bank_filled[bank], before + 1)
                    return ps_bank[:, bank, :]

                m0 = moment0

                def norm_stats(b, arg):
                    dve.wait_ge(x_loaded, 16 * (b + 1))
                    for half in range(halves):
                        last = dve.bn_stats(stat0[:, half, :], x_sb[:, half * HALF:(half + 1) * HALF])
                    mark(last)

                means, spreads = stat0[:, :, 1:6:3], stat0[:, :, 2:6:3]
                parts = 2 * halves

                def norm_means(b, arg):
                    settle()
                    dve.tensor_reduce(m0[:, 2:3], spreads, AXIS.XY, ALU.add)
                    link(dve.tensor_reduce(m0[:, 3:4], means, AXIS.XY, ALU.add))
                    link(dve.tensor_scalar(m0[:, 0:1], m0[:, 3:4], 1.0 / parts, None, ALU.mult))
                    dev = part_dev[:, :].rearrange("p (a b) -> p a b", a=halves)
                    mark(dve.tensor_scalar(dev, means, m0[:, 0:1], None, ALU.subtract))

                def norm_moments(b, arg):
                    settle()
                    link(dve.tensor_tensor(part_dev[:, :], part_dev[:, :], part_dev[:, :], ALU.mult))
                    link(dve.tensor_reduce(m0[:, 4:5], part_dev[:, :], AXIS.X, ALU.add))
                    link(dve.tensor_scalar(m0[:, 4:5], m0[:, 4:5], 1.0 / parts, None, ALU.mult))
                    dve.scalar_tensor_tensor(out=m0[:, 1:2], in0=m0[:, 2:3], scalar=1.0 / tokens, in1=m0[:, 4:5],
                                             op0=ALU.mult, op1=ALU.add).then_inc(moments_ready, 1)

                def norm_group_mean(b, arg):
                    bank = read_bank()
                    dve.tensor_copy(m0[:, 9:11], bank[:, 0:2]).then_inc(mean_read, 1)
                    dve.wait_ge(mean_read, b + 1)
                    link(dve.tensor_tensor(m0[:, 11:12], m0[:, 0:1], m0[:, 9:10], ALU.subtract))
                    dve.tensor_tensor(m0[:, 5:6], m0[:, 11:12], m0[:, 11:12], ALU.mult).then_inc(spread_ready, 1)

                def norm_group_var(b, arg):
                    bank = read_bank()
                    dve.scalar_tensor_tensor(out=m0[:, 7:8], in0=bank[:, 0:1], scalar=EPS, in1=m0[:, 10:11],
                                             op0=ALU.add, op1=ALU.add).then_inc(var_ready[0], 1)

                def norm_apply(b, arg):
                    dve.wait_ge(rstd_ready[0], b + 1)
                    link(dve.tensor_tensor(m0[:, 6:7], m0[:, 8:9], norm_cols[:, 0:1], ALU.mult))
                    link(dve.tensor_tensor(m0[:, 11:12], m0[:, 9:10], m0[:, 6:7], ALU.mult))
                    link(dve.tensor_tensor(m0[:, 11:12], norm_cols[:, 1:2], m0[:, 11:12], ALU.subtract))
                    dve.tensor_scalar(work[:, :], x_sb[:, :], m0[:, 6:7], m0[:, 11:12], ALU.mult, ALU.add)\
                       .then_inc(h_ready, 1)

                def lower_part(hi, lo, layer):
                    def stage(b, arg):
                        order = 0 if hi is q_hi[layer] else halves
                        for half in range(halves):
                            bank = read_bank()
                            dve.wait_ge(hi_ready[layer], 2 * halves * b + order + half + 1)
                            at = slice(half * HALF, (half + 1) * HALF)
                            if layer:
                                last = dve.tensor_tensor(lo[:, at], bank, hi[:, at].bitcast(F32), ALU.subtract)
                            else:
                                bias = qkv_bias[:, 0:1] if hi is q_hi[0] else qkv_bias[:, 1:2]
                                last = dve.scalar_tensor_tensor(out=lo[:, at], in0=bank, scalar=bias,
                                                                in1=hi[:, at].bitcast(F32), op0=ALU.add,
                                                                op1=ALU.subtract)
                            last.then_inc(lo_ready[layer], 1)
                    return stage

                def max0(b, i):
                    for half in range(halves):
                        dve.tensor_reduce(max_part0[:, i, half:half + 1], read_bank(), AXIS.X, ALU.max)\
                           .then_inc(maxed[0], 1)
                    if i == tiles - 1:
                        dve.wait_ge(maxed[0], halves * tiles * (b + 1))
                        dve.tensor_reduce(max_cols0[:, :, 0], max_part0[:, :, :], AXIS.X, ALU.max, negate=True)\
                           .then_inc(max_ready[0], 1)

                def max1(b, arg):
                    phase, use = arg
                    i, n, half = use // (GROUP * halves), use // halves % GROUP, use % halves
                    dve.tensor_reduce(max_part1[:, i, n, half:half + 1], read_bank(), AXIS.X, ALU.max)\
                       .then_inc(maxed[1], 1)
                    if use == uses_per_phase - 1:
                        dve.wait_ge(maxed[1], uses_per_phase * (phases * b + phase + 1))
                        dve.tensor_reduce(max_cols1[:, :, 0:GROUP], max_part1[:, :, :, :], AXIS.X, ALU.max,
                                          negate=True).then_inc(max_ready[1], 1)

                def x_tokens(b, arg):
                    for half in range(halves):
                        bank = read_bank()
                        at = slice(half * tiles_per_half, (half + 1) * tiles_per_half)
                        dve.tensor_tensor(t_front[:, at, :], bank.rearrange("p (i c) -> p i c", c=P),
                                          token_bias[:, :].unsqueeze(1).broadcast_to([P, tiles_per_half, P]),
                                          ALU.add).then_inc(x_used, 1)

                def value0(b, i):
                    if i == 0:
                        dve.wait_ge(x_used, halves * (b + 1))
                    else:
                        dve.wait_ge(value0_added, tiles * b + i)
                        dve.bn_stats(stat1[:, 0, i - 1, :], t_front[:, i - 1, :])
                    bank = read_bank()
                    link(dve.reciprocal(den0[:, i:i + 1], bank[:, P:P + 1]))
                    dve.scalar_tensor_tensor(out=t_front[:, i, :], in0=bank[:, 0:P], scalar=den0[:, i:i + 1],
                                             in1=t_front[:, i, :], op0=ALU.mult, op1=ALU.add)\
                       .then_inc(value0_added, 1)
                    if i == tiles - 1:
                        dve.wait_ge(value0_added, tiles * (b + 1))
                        link(dve.bn_stats(stat1[:, 0, i, :], t_front[:, i, :]))

                def layer_norm_stats(n):
                    def stage(b, arg):
                        m1, stats = moment1, stat1[:, n, :, :]
                        dve.tensor_tensor(m1[:, 0, :], stats[:, :, 1], stats[:, :, 4], ALU.add)
                        dve.tensor_tensor(m1[:, 1, :], stats[:, :, 1], stats[:, :, 4], ALU.subtract)
                        link(dve.tensor_tensor(m1[:, 2, :], stats[:, :, 2], stats[:, :, 5], ALU.add))
                        link(dve.tensor_tensor(m1[:, 3, :], m1[:, 1, :], m1[:, 1, :], ALU.mult))
                        link(dve.tensor_scalar(m1[:, 2, :], m1[:, 2, :], 1.0 / P, EPS, ALU.mult, ALU.add))
                        dve.scalar_tensor_tensor(out=m1[:, 4, :], in0=m1[:, 3, :], scalar=0.25, in1=m1[:, 2, :],
                                                 op0=ALU.mult, op1=ALU.add).then_inc(var_ready[n + 1], 1)
                    return stage

                def layer_norm_shift(n):
                    def stage(b, part):
                        if part:
                            return
                        m1 = moment1
                        dve.wait_ge(rstd_ready[n + 1], b + 1)
                        dve.scalar_tensor_tensor(out=m1[:, 6, :], in0=m1[:, 0, :], scalar=-0.5, in1=m1[:, 5, :],
                                                 op0=ALU.mult, op1=ALU.mult).then_inc(shift_ready[n], 1)
                    return stage

                def turn_sums(b, phase):
                    banks.take()
                    bank = read_bank()
                    den_rows = bank.rearrange("p (m r) -> p m r", r=QUAD)[:, :, 0]
                    dve.tensor_copy(den_tok[:, :], den_rows).then_inc(den_tok_ready, 1)

                def gate_arg(b, phase):
                    group, half = divmod(phase, halves)
                    if phase == 0:
                        dve.wait_ge(rqk_ready, halves * (b + 1))
                    dve.wait_ge(den_tok_ready, phases * b + phase + 1)
                    link(dve.reciprocal(small[:, 0, :], den_tok[:, :]))
                    dve.wait_ge(u_tok_ready, phases * b + phase + 1)
                    keys = rqk[:, half * tiles_per_half:(half + 1) * tiles_per_half,
                               group * GROUP * HEAD_DIM:(group + 1) * GROUP * HEAD_DIM]
                    link(dve.tensor_tensor(prod[:, 0, :, :].rearrange("p (i h) d -> p i h d", h=GROUP),
                                           u_tok[:, :, :, HEAD_DIM:], keys.rearrange("p i (h d) -> p i h d", d=HEAD_DIM),
                                           ALU.mult))
                    link(dve.tensor_reduce(small[:, 1, :], prod[:, 0, :, :], AXIS.X, ALU.add))
                    link(dve.tensor_tensor(small[:, 1, :], small[:, 1, :], small[:, 0, :], ALU.mult))
                    dve.tensor_scalar(small[:, 2, :], small[:, 1, :], -scale1, EXP_ARG_MAX, ALU.mult, ALU.min)\
                       .then_inc(gate_arg_ready, 1)

                def retrieve(b, phase):
                    group, half = divmod(phase, halves)
                    dve.wait_ge(gate_exp_ready, phases * b + phase + 1)
                    link(dve.tensor_scalar(small[:, 4, :], small[:, 3, :], 1.0, None, ALU.add))
                    link(dve.reciprocal(small[:, 5, :], small[:, 4, :]))
                    link(dve.tensor_tensor(small[:, 5, :], small[:, 5, :], small[:, 0, :], ALU.mult))
                    flat = u_tok[:, :, :, :].rearrange("p i h r -> p (i h) r")
                    wide = [P, tiles_per_half * GROUP, HEAD_DIM]
                    dve.tensor_tensor(prod[:, 0, :, :], flat[:, :, 0:HEAD_DIM],
                                      small[:, 0, :].unsqueeze(2).broadcast_to(wide), ALU.mult)
                    link(dve.tensor_tensor(prod[:, 1, :, :], flat[:, :, HEAD_DIM:],
                                           small[:, 5, :].unsqueeze(2).broadcast_to(wide), ALU.mult))
                    if phase == 0:
                        wait(dve, channels_ready[1], halves * b)
                    to = mixed[:, half * tiles_per_half:(half + 1) * tiles_per_half,
                               group * GROUP * HEAD_DIM:(group + 1) * GROUP * HEAD_DIM]
                    dve.tensor_tensor(to.rearrange("p i (h d) -> p i h d", d=HEAD_DIM),
                                      prod[:, 0, :, :].rearrange("p (i h) d -> p i h d", h=GROUP),
                                      prod[:, 1, :, :].rearrange("p (i h) d -> p i h d", h=GROUP),
                                      ALU.add).then_inc(mixed_ready, 1)

                def add_bank(ready):
                    def stage(b, arg):
                        for half in range(halves):
                            bank = read_bank()
                            at = slice(half * tiles_per_half, (half + 1) * tiles_per_half)
                            dve.tensor_tensor(t_core[:, at, :], t_core[:, at, :],
                                              bank.rearrange("p (i c) -> p i c", c=P), ALU.add).then_inc(ready, 1)
                            if ready is out1_added:
                                dve.wait_ge(ready, halves * b + half + 1)
                                for i in range(half * tiles_per_half, (half + 1) * tiles_per_half):
                                    last = dve.bn_stats(stat1[:, 1, i, :], t_core[:, i, :])
                        if ready is out1_added:
                            link(last)
                        else:
                            dve.wait_ge(ready, halves * (b + 1))
                    return stage

                def hold_tokens(b, arg):
                    link(dve.tensor_copy(t_held[:, :, :], t_front[:, :, :]))

                def take_tokens(b, arg):
                    wait(dve, out_ready, halves * b)
                    link(dve.tensor_copy(t_core[:, :, :], t_held[:, :, :]))

                stages = {
                    "norm_stats": norm_stats, "norm_means": norm_means,
                    "norm_moments": norm_moments, "norm_group_mean": norm_group_mean,
                    "norm_group_var": norm_group_var, "norm_apply": norm_apply,
                    "q0": lower_part(q_hi[0], q_lo[0], 0), "k0": lower_part(k_hi[0], k_lo[0], 0),
                    "q1": lower_part(q_hi[1], q_lo[1], 1), "k1": lower_part(k_hi[1], k_lo[1], 1),
                    "max0": max0, "max1": max1,
                    "x_tokens": x_tokens, "value0": value0,
                    "ln1_stats": layer_norm_stats(0), "ln1_apply": layer_norm_shift(0),
                    "ln2_stats": layer_norm_stats(1), "ln2_apply": layer_norm_shift(1),
                   
                    "turn_sums": turn_sums, "gate_arg": gate_arg, "retrieve": retrieve, "out1": add_bank(out1_added),
                    "ffn": add_bank(result_ready), "hold_tokens": hold_tokens,
                    "take_tokens": take_tokens,
                }
                in_order(dve, steps, images, stages, banks, links)

            with nc.Block() as block:
                @block.sync
                def _(sp):
                    sync_program(sp)

                @block.gpsimd
                def _(pool):
                    gpsimd_program(pool)

                @block.tensor
                def _(pe):
                    tensor_program(pe)

                @block.scalar
                def _(act):
                    scalar_program(act)

                @block.vector
                def _(dve):
                    vector_program(dve)

        all_images()


_INS = ["x", "L0_conv_norm_w", "L0_conv_norm_b", "L0_conv_qkv_w", "L0_conv_qkv_b", "L0_conv_proj_w",
        "L0_conv_proj_b", "L1_attn_wq_s", "L1_attn_wk_s", "L1_attn_wv_r", "L1_attn_wq_r", "L1_attn_wk_ret",
        "L1_attn_w_out", "L1_ffn_qidx", "L1_ffn_scales", "L1_ffn_W"]


def kernel(**inputs):
    import concourse.bacc as bacc
    from concourse.bass_utils import run_bass_kernel_spmd

    nc = bacc.Bacc("TRN2", target_bir_lowering=False, num_devices=1)
    arrays, args = {}, []
    for name in _INS:
        a = np.ascontiguousarray(inputs[name])
        arrays[f"in_{name}"] = a
        args.append(nc.dram_tensor(f"in_{name}", a.shape, mybir.dt.from_np(a.dtype), kind="ExternalInput").ap())
    shape = inputs["x"].shape
    args.append(nc.dram_tensor("out_y", shape, F32, kind="ExternalOutput").ap())
    build(nc, *args)
    result = run_bass_kernel_spmd(nc, [arrays], core_ids=[0])
    return result.results[0]["out_y"]
```
